# Optimizing a Trainium2 kernel written in Bass

```python
import numpy as np
import jax
import jax.numpy as jnp

def _softmax(x, axis=-1):
    return jax.nn.softmax(x, axis=axis)

def _gelu(x):
    return jax.nn.gelu(x, approximate=True)

def _silu(x):
    return jax.nn.silu(x)

def _sigmoid(x):
    return jax.nn.sigmoid(x)

def _layernorm(x, axis=-1, eps=1e-05):
    m = jnp.mean(x, axis=axis, keepdims=True)
    v = jnp.var(x, axis=axis, keepdims=True)
    return (x - m) / jnp.sqrt(v + eps)

def _scatter_add(tgt, idx, src, axis=0):
    return tgt.at[idx].add(src)

def _segment_sum(src, seg, n):
    return jax.ops.segment_sum(src, seg, n)
kernel_name = 'mk_seq_postln_d1_jaxref_r4_aea2b0'

def setup_inputs(seed: int=0):
    np.random.seed(seed)
    _w = jnp.asarray

    def _L0_attn_setup():
        import jax, jax.numpy as jnp
        import numpy as np
        B, S, D = (2, 512, 256)
        H, DH = (16, 64)
        DQL, DKVL = (128, 128)
        DR = 64
        TOPK = 64
        LN_EPS = 1e-05
        ROPE_BASE = 10000.0

        def _rope_tables(seq_len, dim):
            inv_freq = 1.0 / ROPE_BASE ** (np.arange(0, dim, 2, dtype=np.float32) / dim)
            t = np.arange(seq_len, dtype=np.float32)
            freqs = np.outer(t, inv_freq)
            cos = np.concatenate([np.cos(freqs), np.cos(freqs)], -1)[:, ::2]
            sin = np.concatenate([np.sin(freqs), np.sin(freqs)], -1)[:, ::2]
            return (jnp.asarray(cos), jnp.asarray(sin))

        def _apply_rope_subspace(x, d_rope):
            s = x.shape[-2]
            cos, sin = _rope_tables(s, d_rope)
            xr, xp = (x[..., :d_rope], x[..., d_rope:])
            e, o = (xr[..., 0::2], xr[..., 1::2])
            rot = jnp.stack([e * cos - o * sin, e * sin + o * cos], axis=-1).reshape(xr.shape)
            return jnp.concatenate([rot, xp], axis=-1)

        def _reference_tuple_inner(x, w_down_q, w_down_kv, w_up_q, w_up_k, w_up_v, w_out, ln_scale, ln_bias):
            b, s, d = x.shape
            residual = x
            mu = jnp.mean(x, axis=-1, keepdims=True)
            var = jnp.mean((x - mu) ** 2, axis=-1, keepdims=True)
            h = (x - mu) * jax.lax.rsqrt(var + LN_EPS) * ln_scale + ln_bias
            c_q = h @ w_down_q.T
            c_kv = h @ w_down_kv.T
            q = (c_q @ w_up_q.T).reshape(b, s, H, DH).transpose(0, 2, 1, 3)
            k = (c_kv @ w_up_k.T).reshape(b, s, H, DH).transpose(0, 2, 1, 3)
            v = (c_kv @ w_up_v.T).reshape(b, s, H, DH).transpose(0, 2, 1, 3)
            q = _apply_rope_subspace(q, DR)
            k = _apply_rope_subspace(k, DR)
            scale = 1.0 / np.sqrt(DH).astype(np.float32)
            scores = jnp.einsum('bhqd,bhkd->bhqk', q, k) * scale
            _, indices = jax.lax.top_k(scores, min(TOPK, s))
            attn = jax.nn.softmax(scores, axis=-1)
            out = jnp.einsum('bhqk,bhkd->bhqd', attn, v)
            out = out.transpose(0, 2, 1, 3).reshape(b, s, H * DH)
            out = out @ w_out.T + residual
            return (out, indices.astype(jnp.int64))
        key = jax.random.key(seed)
        ks = jax.random.split(key, 7)
        init = lambda k, shape: jax.random.normal(k, shape, jnp.float32) * 0.02
        return {'x': jax.random.normal(ks[0], (B, S, D), jnp.float32), 'w_down_q': init(ks[1], (DQL, D)), 'w_down_kv': init(ks[2], (DKVL, D)), 'w_up_q': init(ks[3], (H * DH, DQL)), 'w_up_k': init(ks[4], (H * DH, DKVL)), 'w_up_v': init(ks[5], (H * DH, DKVL)), 'w_out': init(ks[6], (D, H * DH)), 'ln_scale': jnp.ones((D,), jnp.float32), 'ln_bias': jnp.zeros((D,), jnp.float32)}
    _L0_attn_in = _L0_attn_setup()

    def _L0_ffn_setup():
        import jax, jax.numpy as jnp
        import numpy as np
        D_IN, D_HID = (256, 1024)

        def _ternary(key, shape):
            return jax.random.randint(key, shape, -1, 2).astype(jnp.float32)

        def _tlin(x, w, s):
            return jnp.einsum('bsi,oi->bso', x, w) * s
        key = jax.random.key(seed)
        ks = jax.random.split(key, 12)
        inv = lambda fan: 1.0 / np.sqrt(fan).astype(np.float32)
        return {'x': jax.random.normal(ks[0], (4, 512, D_IN), dtype=jnp.float32), 'w1_w': _ternary(ks[1], (D_HID, D_IN)), 'w1_s': jax.random.uniform(ks[2], (D_HID,), dtype=jnp.float32) * inv(D_IN), 'w2_w': _ternary(ks[3], (D_HID, D_IN)), 'w2_s': jax.random.uniform(ks[4], (D_HID,), dtype=jnp.float32) * inv(D_IN), 'h1_w': _ternary(ks[5], (D_HID, D_HID)), 'h1_s': jax.random.uniform(ks[6], (D_HID,), dtype=jnp.float32) * inv(D_HID), 'h2_w': _ternary(ks[7], (D_HID, D_HID)), 'h2_s': jax.random.uniform(ks[8], (D_HID,), dtype=jnp.float32) * inv(D_HID), 'w3_w': _ternary(ks[9], (D_IN, D_HID)), 'w3_s': jax.random.uniform(ks[10], (D_IN,), dtype=jnp.float32) * inv(D_HID)}
    _L0_ffn_in = _L0_ffn_setup()
    _d = {'L0_attn_x': _L0_attn_in['x'], 'L0_attn_w_down_q': _L0_attn_in['w_down_q'], 'L0_attn_w_down_kv': _L0_attn_in['w_down_kv'], 'L0_attn_w_up_q': _L0_attn_in['w_up_q'], 'L0_attn_w_up_k': _L0_attn_in['w_up_k'], 'L0_attn_w_up_v': _L0_attn_in['w_up_v'], 'L0_attn_w_out': _L0_attn_in['w_out'], 'L0_attn_ln_scale': _L0_attn_in['ln_scale'], 'L0_attn_ln_bias': _L0_attn_in['ln_bias'], 'L0_ffn_w1_w': _L0_ffn_in['w1_w'], 'L0_ffn_w1_s': _L0_ffn_in['w1_s'], 'L0_ffn_w2_w': _L0_ffn_in['w2_w'], 'L0_ffn_w2_s': _L0_ffn_in['w2_s'], 'L0_ffn_h1_w': _L0_ffn_in['h1_w'], 'L0_ffn_h1_s': _L0_ffn_in['h1_s'], 'L0_ffn_h2_w': _L0_ffn_in['h2_w'], 'L0_ffn_h2_s': _L0_ffn_in['h2_s'], 'L0_ffn_w3_w': _L0_ffn_in['w3_w'], 'L0_ffn_w3_s': _L0_ffn_in['w3_s']}
    _x0 = _d['L0_attn_x']
    _d['L0_attn_x'] = jax.random.normal(jax.random.fold_in(jax.random.key(seed), 1), (8, 512, 256), dtype=_x0.dtype)
    del _x0
    return _d

def reference(L0_attn_x, L0_attn_w_down_q, L0_attn_w_down_kv, L0_attn_w_up_q, L0_attn_w_up_k, L0_attn_w_up_v, L0_attn_w_out, L0_attn_ln_scale, L0_attn_ln_bias, L0_ffn_w1_w, L0_ffn_w1_s, L0_ffn_w2_w, L0_ffn_w2_s, L0_ffn_h1_w, L0_ffn_h1_s, L0_ffn_h2_w, L0_ffn_h2_s, L0_ffn_w3_w, L0_ffn_w3_s):

    def _L0_attn_ref(x, w_down_q, w_down_kv, w_up_q, w_up_k, w_up_v, w_out, ln_scale, ln_bias):
        import jax, jax.numpy as jnp
        import numpy as np
        B, S, D = (2, 512, 256)
        H, DH = (16, 64)
        DQL, DKVL = (128, 128)
        DR = 64
        TOPK = 64
        LN_EPS = 1e-05
        ROPE_BASE = 10000.0

        def _rope_tables(seq_len, dim):
            inv_freq = 1.0 / ROPE_BASE ** (np.arange(0, dim, 2, dtype=np.float32) / dim)
            t = np.arange(seq_len, dtype=np.float32)
            freqs = np.outer(t, inv_freq)
            cos = np.concatenate([np.cos(freqs), np.cos(freqs)], -1)[:, ::2]
            sin = np.concatenate([np.sin(freqs), np.sin(freqs)], -1)[:, ::2]
            return (jnp.asarray(cos), jnp.asarray(sin))

        def _apply_rope_subspace(x, d_rope):
            s = x.shape[-2]
            cos, sin = _rope_tables(s, d_rope)
            xr, xp = (x[..., :d_rope], x[..., d_rope:])
            e, o = (xr[..., 0::2], xr[..., 1::2])
            rot = jnp.stack([e * cos - o * sin, e * sin + o * cos], axis=-1).reshape(xr.shape)
            return jnp.concatenate([rot, xp], axis=-1)

        def _reference_tuple_inner(x, w_down_q, w_down_kv, w_up_q, w_up_k, w_up_v, w_out, ln_scale, ln_bias):
            b, s, d = x.shape
            residual = x
            mu = jnp.mean(x, axis=-1, keepdims=True)
            var = jnp.mean((x - mu) ** 2, axis=-1, keepdims=True)
            h = (x - mu) * jax.lax.rsqrt(var + LN_EPS) * ln_scale + ln_bias
            c_q = h @ w_down_q.T
            c_kv = h @ w_down_kv.T
            q = (c_q @ w_up_q.T).reshape(b, s, H, DH).transpose(0, 2, 1, 3)
            k = (c_kv @ w_up_k.T).reshape(b, s, H, DH).transpose(0, 2, 1, 3)
            v = (c_kv @ w_up_v.T).reshape(b, s, H, DH).transpose(0, 2, 1, 3)
            q = _apply_rope_subspace(q, DR)
            k = _apply_rope_subspace(k, DR)
            scale = 1.0 / np.sqrt(DH).astype(np.float32)
            scores = jnp.einsum('bhqd,bhkd->bhqk', q, k) * scale
            _, indices = jax.lax.top_k(scores, min(TOPK, s))
            attn = jax.nn.softmax(scores, axis=-1)
            out = jnp.einsum('bhqk,bhkd->bhqd', attn, v)
            out = out.transpose(0, 2, 1, 3).reshape(b, s, H * DH)
            out = out @ w_out.T + residual
            return (out, indices.astype(jnp.int64))
        return _reference_tuple_inner(x, w_down_q, w_down_kv, w_up_q, w_up_k, w_up_v, w_out, ln_scale, ln_bias)[0]

    def _L0_ffn_ref(x, w1_w, w1_s, w2_w, w2_s, h1_w, h1_s, h2_w, h2_s, w3_w, w3_s):
        import jax, jax.numpy as jnp
        import numpy as np
        D_IN, D_HID = (256, 1024)

        def _ternary(key, shape):
            return jax.random.randint(key, shape, -1, 2).astype(jnp.float32)

        def _tlin(x, w, s):
            return jnp.einsum('bsi,oi->bso', x, w) * s
        h = jax.nn.silu(_tlin(x, w1_w, w1_s)) * _tlin(x, w2_w, w2_s)
        h = jax.nn.gelu(_tlin(h, h1_w, h1_s), approximate=False)
        h = jax.nn.gelu(_tlin(h, h2_w, h2_s), approximate=False)
        return _tlin(h, w3_w, w3_s)
    x = L0_attn_x
    x = _layernorm(x + _L0_attn_ref(x, L0_attn_w_down_q, L0_attn_w_down_kv, L0_attn_w_up_q, L0_attn_w_up_k, L0_attn_w_up_v, L0_attn_w_out, L0_attn_ln_scale, L0_attn_ln_bias), axis=-1)
    x = _layernorm(x + _L0_ffn_ref(x, L0_ffn_w1_w, L0_ffn_w1_s, L0_ffn_w2_w, L0_ffn_w2_s, L0_ffn_h1_w, L0_ffn_h1_s, L0_ffn_h2_w, L0_ffn_h2_s, L0_ffn_w3_w, L0_ffn_w3_s), axis=-1)
    return x

_drawn_inputs = setup_inputs


def setup_inputs(seed=0):
    import zlib

    import numpy as np

    out = dict(_drawn_inputs(seed))
    spreads = {'L0_attn_ln_scale': (1.0, 0.6), 'L0_attn_ln_bias': (0.0, 0.8)}
    factors = {'L0_attn_w_down_q': 8.0,
     'L0_attn_w_down_kv': 8.0,
     'L0_attn_w_up_q': 8.0,
     'L0_attn_w_up_k': 8.0,
     'L0_attn_w_up_v': 8.0,
     'L0_attn_w_out': 8.0,
     'L0_ffn_w1_w': 8.0,
     'L0_ffn_w1_s': 8.0,
     'L0_ffn_w2_w': 8.0,
     'L0_ffn_w2_s': 8.0,
     'L0_ffn_h1_w': 8.0,
     'L0_ffn_h1_s': 8.0,
     'L0_ffn_h2_w': 8.0,
     'L0_ffn_h2_s': 8.0,
     'L0_ffn_w3_w': 8.0,
     'L0_ffn_w3_s': 8.0}
    for name, (base, spread) in spreads.items():
        noise = np.random.default_rng([zlib.crc32(name.encode()), seed]).standard_normal(out[name].shape)
        drawn = base * np.exp(spread * noise) if base else spread * noise
        out[name] = jnp.asarray(drawn.astype(out[name].dtype))
    for name, factor in factors.items():
        out[name] = (out[name] * factor).astype(out[name].dtype)
    return out
```

```python
from contextlib import ExitStack

import numpy as np

import concourse.bass as bass
from concourse import mybir

F32 = mybir.dt.float32
F32R = mybir.dt.float32r
I32 = mybir.dt.int32
ACT = mybir.ActivationFunctionType
ALU = mybir.AluOpType
AX = mybir.AxisListType

P = 128
NB, S, D = 8, 512, 256
H, DH = 16, 64
L = 128
F = 1024
TT = S // P
DT = D // P
FT = F // P
NG, GH = 4, 4
HP = H // 2
EPS = 1e-5
RSQRT_MAGIC = 1597463007.0
NEWTON = 3
LN_STEPS = 2 * TT + 2 + 4 * NEWTON + TT

PROLOGUE = ([("hT", 0), ("hT", 1), ("c", 0), ("c", 1)] + [("v", t, 0) for t in range(TT)]
            + [("qk", w, e, g) for g in range(2) for w in range(2) for e in range(2)])
PER_SEQ = {"hT": DT, "c": 2, "v": 2 * TT, "qk": 4 * NG, "rb": HP, "ot": DT, "ob": TT // 2}


def nth(b, key):
    what = key[0]
    at = {"v": lambda t, half: TT * half + t, "qk": lambda w, e, g: 4 * g + 2 * w + e}.get(what, lambda i: i)(*key[1:])
    return PER_SEQ[what] * b + (at + 1)


def qk(w, g):
    return [("qk", w, 0, g), ("qk", w, 1, g)]


SCHED = [
    ([], [("rb", 7), ("ot", 0)], [("ot", 1)]),
    ([("ob", 0)], [("ob", 1)], []),
    (qk(0, 2), [("rb", 0)], []),
    (qk(1, 2), [], []),
    ([("rb", 1)], [("v", 0, 1)], [("v", 1, 1)]),
    ([], [("v", 2, 1)], [("v", 3, 1)]),
    (qk(0, 3), [("rb", 2)], []),
    (qk(1, 3), [("hT", 0)], [("hT", 1)]),
    ([("rb", 3)], [("c", 0)], [("c", 1)]),
    ([], [], []),
    (qk(0, 0), [("rb", 4)], []),
    (qk(1, 0), [("v", 0, 0)], []),
    ([("rb", 5)], [("v", 1, 0)], [("v", 2, 0)]),
    ([], [("v", 3, 0)], []),
    (qk(0, 1), [("rb", 6)], []),
    (qk(1, 1), [], []),
]
LN1_STEP, LN2_STEP = 5, 1
OF_PREV = [("rb", 7), ("ot", 0), ("ot", 1), ("ob", 0), ("ob", 1)]
OF_NEXT = PROLOGUE
LAST_USE = [key for places in SCHED for place in places for key in place][-1]

SLOTS = 2 * GH
QK_READS = 4


def build(nc, x, w_dn, w_upq, w_upk, w_upv, w_o, ln_sb, rope, w1, w2, wh1, wh2, w3, s1, s2, sh1, sh2, s3, out):
    x1_dram = nc.dram_tensor("x1_dram", (NB, P, TT * D), F32, kind="Internal").ap()
    ident_sem = nc.alloc_semaphore("ident_built")
    with ExitStack() as keep:
        ident = keep.enter_context(nc.sbuf_tensor("ident", [P, P], F32))
        attention(nc, x, w_dn, w_upq, w_upk, w_upv, w_o, ln_sb, rope, x1_dram, ident, ident_sem)
        ffn(nc, x1_dram, w1, w2, wh1, wh2, w3, s1, s2, sh1, sh2, s3, out, ident)


def layernorm(nc, dve, rows, dst, stats, mv, ve, y, t, chain, base):
    n = [0]

    def link(ins, wait=True):
        n[0] += 1
        ins.then_inc(chain, 1)
        if wait:
            dve.wait_ge(chain, base + n[0])

    for i in range(TT):
        link(nc.vector.bn_stats(stats[:, i, :], rows[:, i, :]), wait=i == TT - 1)
    nc.vector.memset(t[:], 0.0)
    for i in range(TT):
        link(nc.vector.bn_aggr(mv[:, i, :], stats[:, i, :]), wait=i == TT - 1)
    link(nc.vector.tensor_scalar(ve[:], mv[:, :, 1], EPS, None, ALU.add))
    link(nc.vector.tensor_scalar(y[:].bitcast(I32), ve[:].bitcast(I32), -0.5, RSQRT_MAGIC, ALU.mult, ALU.add))
    for _ in range(NEWTON):
        link(nc.vector.tensor_tensor(t[:], y[:], y[:], ALU.mult))
        link(nc.vector.tensor_tensor(t[:], t[:], ve[:], ALU.mult))
        link(nc.vector.tensor_scalar(t[:], t[:], -0.5, 1.5, ALU.mult, ALU.add))
        link(nc.vector.tensor_tensor(y[:], y[:], t[:], ALU.mult))
    for i in range(TT):
        link(nc.vector.tensor_scalar(dst[:, i, :], rows[:, i, :], mv[:, i, 0:1], y[:, i:i + 1],
                                     ALU.subtract, ALU.mult), wait=False)
    assert n[0] == LN_STEPS


def attention(nc, x, w_dn, w_upq, w_upk, w_upv, w_o, ln_sb, rope, x1_dram, ident, ident_built):
    with ExitStack() as ctx:
        def sb(name, shape, dt=F32):
            return ctx.enter_context(nc.sbuf_tensor(name, shape, dt))

        def psum(name, shape):
            return ctx.enter_context(nc.psum_tensor(name, shape, F32))

        def sem(name):
            return ctx.enter_context(nc.semaphore(name))

        wdn = sb("wdn", [P, DT, 2 * L])
        wqk_hi = sb("wqk_hi", [P, 2, H * DH], F32R)
        wqk_lo = sb("wqk_lo", [P, 2, H * DH], F32R)
        wv_hi = sb("wv_hi", [P, H * DH], F32R)
        wv_lo = sb("wv_lo", [P, H * DH], F32R)
        wo = sb("wo", [P, HP, D])
        lnsb = sb("lnsb", [P, 2, DT])
        cs = sb("cs", [P, 2, S])
        xn = sb("xn", [P, TT, D])
        xr = sb("xr", [P, TT, D])
        c_hi = sb("c_hi", [P, 2, S], F32R)
        c_lo = sb("c_lo", [P, 2, S], F32R)
        rm = sb("rm", [P, 4, S])
        hl = sb("hl", [P, 2, 2, S], F32R)
        q_st = sb("q_st", [P, SLOTS, S], F32R)
        k_st = sb("k_st", [P, SLOTS, 2, S], F32R)
        v_st = sb("v_st", [P, TT, H, 2 * DH], F32R)
        ex = sb("ex", [P, 2, TT, S])
        pt_hi = sb("pt_hi", [P, 2, S], F32R)
        pt_lo = sb("pt_lo", [P, 2, S], F32R)
        ua = sb("ua", [P, S])
        ub = sb("ub", [P, S])
        at = sb("at", [P, HP, S])
        negmax = sb("negmax", [P, 2, TT])
        rsum = sb("rsum", [P, H, TT])
        rinv = sb("rinv", [P, H, TT])
        rinv_b = sb("rinv_b", [P, TT, 2, DH])
        ln_t = [sb(f"ln_{n}", s) for n, s in (("st", [P, TT, 6]), ("mv", [P, TT, 2]), ("ve", [P, TT]),
                                              ("y", [P, TT]), ("t", [P, TT]))]
        hT = sb("hT", [P, DT, S])
        raw = at

        ps_s = psum("ps_s", [P, TT, S])
        ps_t = psum("ps_t", [P, 2, S])
        ps_v = psum("ps_v", [P, S])
        ps_m = psum("ps_m", [P, S])

        w_loaded = sem("w_loaded")
        up_loaded = [sem(f"up{i}_loaded") for i in range(3)]
        w_hi_done = sem("w_hi_done")
        w_lo_done = sem("w_lo_done")
        xn_loaded = sem("xn_loaded")
        xr_loaded = sem("xr_loaded")
        ln1_chain = sem("ln1_chain")
        ln2_chain = sem("ln2_chain")
        x1_stored = sem("x1_stored")
        ready = {what: sem(f"{what}_ready") for what in PER_SEQ}
        done = {what: sem(f"{what}_done") for what in PER_SEQ}
        c_hi_done = sem("c_hi_done")
        v_hi_done = sem("v_hi_done")
        rope_add = sem("rope_add")
        rope_hi = sem("rope_hi")
        rope_lo = sem("rope_lo")
        parked = sem("parked")
        placed = [[sem(f"placed_{n}{s}") for s in range(2)] for n in "qk"]
        s_ready = sem("s_ready")
        max_done = sem("max_done")
        exp_done = sem("exp_done")
        t_ready = sem("t_ready")
        pt_hi_done = sem("pt_hi_done")
        pt_lo_done = sem("pt_lo_done")
        pv_done = sem("pv_done")
        pv_copied = sem("pv_copied")
        u_summed = sem("u_summed")
        rinv_done = sem("rinv_done")
        rinv_b_done = sem("rinv_b_done")

        park = [[nc.dram_tensor(f"park_{n}{i}", (P, 4 * S), F32, kind="Internal").ap() for i in range(2)] for n in "qk"]
        x_v = x.rearrange("b (t p) d -> b p t d", p=P)
        x1_v = x1_dram.rearrange("b p (t d) -> b p t d", t=TT)

        def seqs(eng, body, prologue, epilogue):
            prologue()
            body(0, first=True)
            with eng.Fori(1, NB - 1) as b:
                body(b)
            body(NB - 1, last=True)
            epilogue()

        def keys(h, place, first, last):
            for key in SCHED[h][place]:
                of = -1 if key in OF_PREV else 1 if key in OF_NEXT else 0
                if not (first and of < 0) and not (last and of > 0):
                    yield key, of

        block = ctx.enter_context(nc.Block())

        @block.sync
        def _(sp):
            def moves(b, w, g):
                sp.wait_ge(rope_lo, 2 * NG * b + (2 * g + w + 1))
                spot = park[w][g % 2]
                sp.dma_start(spot, hl[:].rearrange("p e a s -> p (e a s)").bitcast(F32)).then_inc(parked, 16)
                sp.wait_ge(parked, 32 * NG * b + 16 * (2 * g + w + 1))
                s0 = GH * (g % 2)
                blocks = spot.rearrange("(j r) (e a s) -> a e r j s", j=GH, a=2, e=2)
                both = spot.rearrange("(j r) (e z) -> e r j z", j=GH, e=2)
                for half in range(2):
                    for e in range(2):
                        r0 = 64 * half + 32 * e
                        if w == 0:
                            sp.dma_start(q_st[r0:r0 + 32, s0:s0 + GH, :].bitcast(F32),
                                         blocks[half, e]).then_inc(placed[w][g % 2], 16)
                        else:
                            sp.dma_start(k_st[r0:r0 + 32, s0:s0 + GH].rearrange("r j a s -> r j (a s)").bitcast(F32),
                                         both[e]).then_inc(placed[w][g % 2], 16)

            def load_xn(b):
                sp.dma_start(xn[:], x_v[b]).then_inc(xn_loaded, 16)

            def load_xr(b):
                sp.dma_start(xr[:], x_v[b]).then_inc(xr_loaded, 16)

            def prologue():
                sp.dma_start(xn[:], x_v[0]).then_inc(xn_loaded, 16)
                sp.dma_start(lnsb[:], ln_sb).then_inc(w_loaded, 16)
                sp.dma_start(wdn[:], w_dn.rearrange("(k p) n -> p k n", p=P)).then_inc(w_loaded, 16)
                for i, w in enumerate((w_upq, w_upk, w_upv)):
                    sp.dma_start(raw[:, 2 * i:2 * i + 2, :], w.rearrange("p (a s) -> p a s", s=S)).then_inc(up_loaded[i], 16)
                sp.dma_start(cs[:], rope).then_inc(w_loaded, 16)
                sp.dma_start(wo[:], w_o.rearrange("(k p) n -> p k n", p=P)).then_inc(w_loaded, 16)
                load_xr(0)
                sp.wait_ge(done["hT"], DT)
                load_xn(1)
                for g in range(2):
                    for w in range(2):
                        moves(0, w, g)

            def store_x1(b):
                sp.wait_ge(ln2_chain, LN_STEPS * (b + 1))
                sp.dma_start(x1_v[b], xr[:]).then_inc(x1_stored, 16)

            def body(b, first=False, last=False):
                for h in range(H):
                    if h == 0 and not last and not first:
                        sp.wait_ge(done["hT"], DT * b + DT)
                        load_xn(b + 1)
                    if h == 2 and not first:
                        store_x1(b - 1)
                    if h == 3 and not first:
                        sp.wait_ge(x1_stored, 16 * b)
                        load_xr(b)
                    for place in range(3):
                        for key, of in keys(h, place, first, last):
                            if key[0] == "qk" and key[2] == 1:
                                moves(b + of, key[1], key[3])

            def epilogue():
                store_x1(NB - 1)
                sp.wait_ge(x1_stored, 16 * NB)

            seqs(sp, body, prologue, epilogue)

        @block.tensor
        def _(pe):
            before = [None]

            def misc(b, key):
                if before[0]:
                    pe.wait_ge(done[before[0][1][0]], nth(*before[0]))
                before[0] = (b, key)
                what = key[0]
                if what == "hT":
                    pe.wait_ge(ln1_chain, LN_STEPS * (b + 1))
                    for t in range(TT):
                        ins = nc.tensor.transpose(ps_m[:, t * P:(t + 1) * P], xn[:, t, key[1] * P:(key[1] + 1) * P], ident[:])
                elif what == "c":
                    pe.wait_ge(done["hT"], DT * b + DT)
                    for k in range(DT):
                        ins = nc.tensor.matmul(ps_m[:], wdn[:, k, key[1] * L:(key[1] + 1) * L], hT[:, k, :],
                                               start=k == 0, stop=k == DT - 1)
                elif what == "v":
                    pe.wait_ge(done["c"], 2 * b + 2)
                    t, half = key[1], key[2]
                    lhs = (c_hi, c_hi, c_lo)
                    rhs = (wv_hi, wv_lo, wv_hi)
                    for i in range(3):
                        ins = nc.tensor.matmul(ps_m[:], lhs[i][:, 1, t * P:(t + 1) * P],
                                               rhs[i][:, half * S:(half + 1) * S], start=i == 0, stop=i == 2)
                elif what == "qk":
                    pe.wait_ge(done["c"], 2 * b + 2)
                    w, e, g = key[1:]
                    col = (2 * g + e) * P
                    lhs = (wqk_hi, wqk_lo, wqk_hi)
                    rhs = (c_hi, c_hi, c_lo)
                    for i in range(3):
                        ins = nc.tensor.matmul(ps_m[:], lhs[i][:, w, col:col + P], rhs[i][:, w, :],
                                               start=i == 0, stop=i == 2)
                elif what == "rb":
                    p = key[1]
                    pe.wait_ge(rinv_b_done, HP * b + p + 1)
                    for t in range(TT):
                        ins = nc.tensor.transpose(ps_m[:, t * P:(t + 1) * P],
                                                  rinv_b[:, t].rearrange("p h d -> p (h d)"), ident[:])
                elif what == "ot":
                    pe.wait_ge(done["rb"], HP * b + HP)
                    for p in range(HP):
                        ins = nc.tensor.matmul(ps_m[:], wo[:, p, key[1] * P:(key[1] + 1) * P], at[:, p, :],
                                               start=p == 0, stop=p == HP - 1)
                elif what == "ob":
                    pe.wait_ge(done["ot"], DT * b + DT)
                    for i in range(2):
                        t = 2 * key[1] + i
                        for d in range(DT):
                            ins = nc.tensor.transpose(ps_m[:, i * D + d * P:i * D + (d + 1) * P],
                                                      hT[:, d, t * P:(t + 1) * P], ident[:])
                ins.then_inc(ready[what], 1)

            def scores(b, h, pair):
                slot, g = h % SLOTS, h // GH
                if pair == 0 and h % GH == 0:
                    for w in range(2):
                        pe.wait_ge(placed[w][g % 2], 16 * QK_READS * (NG // 2 * b + (g // 2 + 1)))
                if h > 0:
                    pe.wait_ge(exp_done, TT * H * b + TT * (h - 1) + 2 * pair + 2)
                elif not (isinstance(b, int) and b == 0):
                    pe.wait_ge(exp_done, TT * H * b + (2 * pair - 2))
                for i in range(2):
                    t = 2 * pair + i
                    for part in range(2):
                        ins = nc.tensor.matmul(ps_s[:, t, :], q_st[:, slot, t * P:(t + 1) * P], k_st[:, slot, part, :],
                                               start=part == 0, stop=part == 1)
                ins.then_inc(s_ready, 1)

            def transposes(b, h, kt):
                n = TT * h + kt
                if kt == 0:
                    pe.wait_ge(exp_done, TT * H * b + TT * (h + 1))
                if n >= 2:
                    pe.wait_ge(pt_lo_done, TT * H * b + n - 1)
                for t in range(TT):
                    ins = nc.tensor.transpose(ps_t[:, kt % 2, t * P:(t + 1) * P], ex[:, h % 2, t, kt * P:(kt + 1) * P], ident[:])
                ins.then_inc(t_ready, 1)

            def values(b, h, kt):
                if kt == 0:
                    pe.wait_ge(pv_copied, H * b + h)
                    if h == 0:
                        pe.wait_ge(done["v"], 2 * TT * b + TT)
                    if h == H // 2:
                        pe.wait_ge(done["v"], 2 * TT * b + 2 * TT)
                pe.wait_ge(pt_lo_done, TT * H * b + TT * h + kt + 1)
                nc.tensor.matmul(ps_v[:], v_st[:, kt, h, :], pt_hi[:, kt % 2, :], start=kt == 0, stop=False)
                nc.tensor.matmul(ps_v[:], v_st[:, kt, h, :], pt_lo[:, kt % 2, :], start=False,
                                 stop=kt == TT - 1).then_inc(pv_done, 1)

            def prologue():
                pe.wait_ge(ident_built, 2)
                pe.wait_ge(w_loaded, 64)
                pe.wait_ge(w_lo_done, 3)
                for key in PROLOGUE:
                    misc(0, key)
                scores(0, 0, 0)
                scores(0, 0, 1)

            def body(b, first=False, last=False):
                if not first:
                    before[0] = (b, LAST_USE)

                def place(h, i):
                    for key, of in keys(h, i, first, last):
                        misc(b + of, key)

                def next_scores(h, pair):
                    if h + 1 < H:
                        scores(b, h + 1, pair)
                    elif not last:
                        scores(b + 1, 0, pair)

                for h in range(H):
                    next_scores(h, 0)
                    transposes(b, h, 0)
                    transposes(b, h, 1)
                    place(h, 0)
                    next_scores(h, 1)
                    values(b, h, 0)
                    transposes(b, h, 2)
                    place(h, 1)
                    values(b, h, 1)
                    transposes(b, h, 3)
                    values(b, h, 2)
                    place(h, 2)
                    values(b, h, 3)

            def epilogue():
                for key in OF_PREV:
                    misc(NB - 1, key)

            seqs(pe, body, prologue, epilogue)

        @block.scalar
        def _(act):
            def exps(b, h, pair):
                act.wait_ge(max_done, 2 * H * b + (2 * h + pair + 1))
                for t in (2 * pair, 2 * pair + 1):
                    nc.scalar.activation(ex[:, h % 2, t, :], ps_s[:, t, :], ACT.Exp, bias=negmax[:, h % 2, t:t + 1],
                                         accum_out=rsum[:, h, t:t + 1]).then_inc(exp_done, 1)

            def pt_his(b, h, kt):
                n = TT * h + kt
                act.wait_ge(t_ready, TT * H * b + (n + 1))
                if n >= 2:
                    act.wait_ge(pv_done, TT * H * b + (n - 1))
                nc.scalar.activation(pt_hi[:, kt % 2, :], ps_t[:, kt % 2, :], ACT.Copy).then_inc(pt_hi_done, 1)

            def copy_pv(b, h):
                act.wait_ge(pv_done, TT * H * b + (TT * h + TT))
                act.wait_ge(done["rb"], HP * b + h // 2)
                r = DH * (h % 2)
                nc.scalar.activation(ua[r:r + DH, :], ps_v[0:DH, :], ACT.Copy)
                nc.scalar.activation(ub[r:r + DH, :], ps_v[DH:2 * DH, :], ACT.Copy).then_inc(pv_copied, 1)

            def rope_his(b, w, g):
                act.wait_ge(rope_add, 2 * NG * b + (2 * g + w + 1))
                act.wait_ge(parked, 32 * NG * b + 16 * (2 * g + w))
                nc.scalar.activation(hl[:, :, 0, :], rm[:, 0:2, :], ACT.Copy).then_inc(rope_hi, 1)

            def misc(b, key):
                what = key[0]
                if what in ("c", "v", "ot"):
                    act.wait_ge(ready[what], nth(b, key))
                if what == "c":
                    nc.scalar.activation(c_hi[:, key[1], :], ps_m[:], ACT.Copy).then_inc(c_hi_done, 1)
                elif what == "v":
                    t, half = key[1:]
                    nc.scalar.activation(v_st[:, t, half * (H // 2):(half + 1) * (H // 2), 0:DH],
                                         ps_m[:].rearrange("p (h d) -> p h d", d=DH), ACT.Copy).then_inc(v_hi_done, 1)
                elif what == "ot":
                    nc.scalar.activation(hT[:, key[1], :], ps_m[:], ACT.Copy).then_inc(done["ot"], 1)

            def prologue():
                for key in PROLOGUE:
                    misc(0, key)
                    if key[0] == "qk" and key[2] == 1:
                        rope_his(0, key[1], key[3])
                exps(0, 0, 0)
                exps(0, 0, 1)

            def body(b, first=False, last=False):
                def place(h, i):
                    for key, of in keys(h, i, first, last):
                        misc(b + of, key)

                def next_exps(h, pair):
                    if h + 1 < H:
                        exps(b, h + 1, pair)
                    elif not last:
                        exps(b + 1, 0, pair)

                for h in range(H):
                    if h > 0:
                        copy_pv(b, h - 1)
                    elif not first:
                        copy_pv(b - 1, H - 1)
                    pt_his(b, h, 0)
                    pt_his(b, h, 1)
                    place(h, 0)
                    next_exps(h, 0)
                    pt_his(b, h, 2)
                    place(h, 1)
                    pt_his(b, h, 3)
                    next_exps(h, 1)
                    place(h, 2)
                    for i in range(3):
                        for key, of in keys(h, i, first, last):
                            if key[0] == "qk" and key[2] == 1:
                                rope_his(b + of, key[1], key[3])

            def epilogue():
                copy_pv(NB - 1, H - 1)
                for key in OF_PREV:
                    misc(NB - 1, key)

            seqs(act, body, prologue, epilogue)

        @block.vector
        def _(dve):
            def maxes(b, h, pair):
                dve.wait_ge(s_ready, 2 * H * b + (2 * h + pair + 1))
                nc.vector.tensor_reduce(negmax[:, h % 2, 2 * pair:2 * pair + 2], ps_s[:, 2 * pair:2 * pair + 2, :],
                                        AX.X, ALU.max, negate=True).then_inc(max_done, 1)

            def pt_los(b, h, kt):
                dve.wait_ge(pt_hi_done, TT * H * b + (TT * h + kt + 1))
                nc.vector.tensor_tensor(pt_lo[:, kt % 2, :], ps_t[:, kt % 2, :], pt_hi[:, kt % 2, :].bitcast(F32),
                                        ALU.subtract).then_inc(pt_lo_done, 1)

            def rinvs(b, p):
                dve.wait_ge(exp_done, TT * H * b + TT * 2 * (p + 1))
                r = rinv[:, 2 * p:2 * p + 2, :]
                nc.vector.reciprocal(r, rsum[:, 2 * p:2 * p + 2, :]).then_inc(rinv_done, 1)
                dve.wait_ge(rinv_done, HP * b + (p + 1))
                nc.vector.tensor_copy(rinv_b[:], r.rearrange("p h t -> p t h").unsqueeze(3).broadcast_to([P, TT, 2, DH])
                                      ).then_inc(rinv_b_done, 1)

            def misc(b, key):
                what = key[0]
                if what != "ot":
                    dve.wait_ge(ready[what], nth(b, key))
                if what == "hT":
                    d = key[1]
                    nc.vector.tensor_scalar(hT[:, d, :], ps_m[:], lnsb[:, 0, d:d + 1], lnsb[:, 1, d:d + 1],
                                            ALU.mult, ALU.add).then_inc(done["hT"], 1)
                elif what == "c":
                    dve.wait_ge(c_hi_done, 2 * b + (key[1] + 1))
                    nc.vector.tensor_tensor(c_lo[:, key[1], :], ps_m[:], c_hi[:, key[1], :].bitcast(F32),
                                            ALU.subtract).then_inc(done["c"], 1)
                elif what == "v":
                    t, half = key[1:]
                    dve.wait_ge(v_hi_done, nth(b, key))
                    heads = slice_of(half)
                    nc.vector.tensor_tensor(v_st[:, t, heads[0]:heads[1], DH:2 * DH],
                                            ps_m[:].rearrange("p (h d) -> p h d", d=DH),
                                            v_st[:, t, heads[0]:heads[1], 0:DH].bitcast(F32),
                                            ALU.subtract).then_inc(done["v"], 1)
                elif what == "qk":
                    w, e, g = key[1:]
                    if e == 0:
                        dve.wait_ge(rope_lo, 2 * NG * b + (2 * g + w))
                        a0, a1 = (0, 0), (1, 1)
                    else:
                        a0, a1 = (2, 1), (3, 0)
                    nc.vector.tensor_tensor(rm[:, a0[0], :], ps_m[:], cs[:, a0[1], :], ALU.mult)
                    nc.vector.tensor_tensor(rm[:, a1[0], :], ps_m[:], cs[:, a1[1], :], ALU.mult).then_inc(done["qk"], 1)
                elif what == "rb":
                    p = key[1]
                    dve.wait_ge(u_summed, HP * b + (p + 1))
                    nc.vector.tensor_tensor(at[:, p, :], ps_m[:], ua[:], ALU.mult).then_inc(done["rb"], 1)
                elif what == "ob":
                    u = key[1]
                    dve.wait_ge(xr_loaded, 16 * b + 16)
                    v = xr[:, 2 * u:2 * u + 2, :].rearrange("p t d -> p (t d)")
                    nc.vector.scalar_tensor_tensor(out=v, in0=v, scalar=2.0, in1=ps_m[:], op0=ALU.mult,
                                                   op1=ALU.add).then_inc(done["ob"], 1)

            def ln1(b):
                dve.wait_ge(xn_loaded, 16 * b + 16)
                layernorm(nc, dve, xn, xn, *ln_t, ln1_chain, LN_STEPS * b)

            def ln2(b):
                dve.wait_ge(done["ob"], 2 * b + 2)
                layernorm(nc, dve, xr, xr, *ln_t, ln2_chain, LN_STEPS * b)

            def prologue():
                for i, (hi, lo, scale) in enumerate(((wqk_hi[:, 0], wqk_lo[:, 0], DH ** -0.5),
                                                     (wqk_hi[:, 1], wqk_lo[:, 1], 1.0), (wv_hi[:], wv_lo[:], 1.0))):
                    dve.wait_ge(up_loaded[i], 16)
                    r = raw[:, 2 * i:2 * i + 2, :].rearrange("p a s -> p (a s)")
                    nc.vector.tensor_scalar(hi, r, scale, None, ALU.mult).then_inc(w_hi_done, 1)
                    dve.wait_ge(w_hi_done, i + 1)
                    nc.vector.scalar_tensor_tensor(out=lo, in0=r, scalar=scale, in1=hi.bitcast(F32), op0=ALU.mult,
                                                   op1=ALU.subtract).then_inc(w_lo_done, 1)
                ln1(0)
                dve.wait_ge(w_loaded, 64)
                for key in PROLOGUE:
                    misc(0, key)
                maxes(0, 0, 0)
                maxes(0, 0, 1)

            def body(b, first=False, last=False):
                def place(h, i):
                    for key, of in keys(h, i, first, last):
                        misc(b + of, key)

                def next_maxes(h, pair):
                    if h + 1 < H:
                        maxes(b, h + 1, pair)
                    elif not last:
                        maxes(b + 1, 0, pair)

                for h in range(H):
                    next_maxes(h, 0)
                    pt_los(b, h, 0)
                    pt_los(b, h, 1)
                    if h % 2 == 1:
                        rinvs(b, h // 2)
                    place(h, 0)
                    next_maxes(h, 1)
                    pt_los(b, h, 2)
                    place(h, 1)
                    pt_los(b, h, 3)
                    place(h, 2)
                    if h == LN2_STEP and not first:
                        ln2(b - 1)
                    if h == LN1_STEP and not last:
                        ln1(b + 1)

            def epilogue():
                for key in OF_PREV:
                    misc(NB - 1, key)
                ln2(NB - 1)

            seqs(dve, body, prologue, epilogue)

        @block.gpsimd
        def _(pool):
            def add_parts(b, p):
                pool.wait_ge(pv_copied, H * b + (2 * p + 2))
                nc.gpsimd.tensor_tensor(ua[:], ua[:], ub[:], ALU.add).then_inc(u_summed, 1)

            def rotate(b, w, g):
                pool.wait_ge(done["qk"], nth(b, ("qk", w, 1, g)))
                nc.gpsimd.tensor_tensor(rm[:, 0, :], rm[:, 0, :], rm[:, 2, :], ALU.subtract)
                nc.gpsimd.tensor_tensor(rm[:, 1, :], rm[:, 1, :], rm[:, 3, :], ALU.add).then_inc(rope_add, 1)
                pool.wait_ge(rope_hi, 2 * NG * b + (2 * g + w + 1))
                nc.gpsimd.tensor_tensor(hl[:, :, 1, :], rm[:, 0:2, :], hl[:, :, 0, :].bitcast(F32),
                                        ALU.subtract).then_inc(rope_lo, 1)

            def prologue():
                nc.gpsimd.memset(ident[:], 0.0).then_inc(ident_built, 1)
                pool.wait_ge(ident_built, 1)
                nc.gpsimd.affine_select(out=ident[:], in_=ident[:], compare_op=ALU.not_equal, fill=1.0, base=0,
                                        pattern=[[-1, P]], channel_multiplier=1).then_inc(ident_built, 1)
                for g in range(2):
                    for w in range(2):
                        rotate(0, w, g)

            def body(b, first=False, last=False):
                for h in range(H):
                    if h % 2 == 0 and h > 0:
                        add_parts(b, h // 2 - 1)
                    elif h == 0 and not first:
                        add_parts(b - 1, HP - 1)
                    for i in range(3):
                        for key, of in keys(h, i, first, last):
                            if key[0] == "qk" and key[2] == 1:
                                rotate(b + of, key[1], key[3])

            def epilogue():
                add_parts(NB - 1, HP - 1)

            seqs(pool, body, prologue, epilogue)


def slice_of(half):
    return half * (H // 2), (half + 1) * (H // 2)


def ffn(nc, x1_dram, w1, w2, wh1, wh2, w3, s1, s2, sh1, sh2, s3, out, ident):
    with ExitStack() as ctx:
        def sb(name, shape, dt=F32):
            return ctx.enter_context(nc.sbuf_tensor(name, shape, dt))

        def sem(name):
            return ctx.enter_context(nc.semaphore(name))

        w12 = [sb("w1_sb", [P, DT, F]), sb("w2_sb", [P, DT, F])]
        wh = [sb("wh1_sb", [P, FT, F]), sb("wh2_sb", [P, FT, F])]
        w3_sb = sb("w3_sb", [P, FT, D])
        sc = sb("sc", [P, 4, FT])
        s3_sb = sb("s3_sb", [P, DT])
        xf = [sb(f"xf{i}", [P, TT, D]) for i in range(2)]
        xT = sb("xT", [P, DT, S])
        gate = sb("gate", [P, 2, S])
        act_a = sb("act_a", [P, FT, S])
        act_b = sb("act_b", [P, FT, S])
        yT = sb("yT", [P, DT, S])
        ln_t = [sb(f"lnf_{n}", s) for n, s in (("st", [P, TT, 6]), ("mv", [P, TT, 2]), ("ve", [P, TT]),
                                               ("y", [P, TT]), ("t", [P, TT]))]
        NBK = 4
        bank = ctx.enter_context(nc.psum_tensor("bank", [P, NBK, S], F32))

        uses = ([(("xT", d), "act") for d in range(DT)]
                + [((f"w{i + 1}", m), ("act", "dve")[i]) for m in range(FT) for i in range(2)]
                + [(("h1", m), "act") for m in range(FT)] + [(("h2", m), "act") for m in range(FT)]
                + [(("w3", d), "act") for d in range(DT)] + [(("back", u), "dve") for u in range(TT // 2)])
        NU = len(uses)
        number = {key: n for n, (key, _) in enumerate(uses)}
        assert (2 * NU) % NBK == 0
        per_seq = {r: sum(1 for _, who in uses if who == r) for r in ("act", "dve")}
        reads = [sum(1 for _, who in uses[:n + 1] if who == uses[n][1]) for n in range(NU)]

        wf_loaded = [sem(f"wf{i}_loaded") for i in range(5)]
        sc_loaded = sem("sc_loaded")
        xf_loaded = [sem(f"xf{i}_loaded") for i in range(2)]
        stored = sem("stored")
        filled = sem("filled")
        read = {"act": sem("act_read"), "dve": sem("dve_read")}
        ln_chain = sem("lnf_chain")

        x1_v = x1_dram.rearrange("b p (t d) -> b p t d", t=TT)
        out_v = out.rearrange("b (t p) d -> b p t d", p=P)
        block = ctx.enter_context(nc.Block())

        def pairs(eng, seq):
            seq(0, 0, 0)
            seq(1, 1, 0)
            with eng.Fori(1, NB // 2) as i:
                for u in range(2):
                    seq(2 * i + u, u, i)

        def bank_of(u, key):
            return bank[:, (NU * u + number[key]) % NBK, :]

        def reader_count(b, key):
            return per_seq[uses[number[key]][1]] * b + reads[number[key]]

        @block.sync
        def _(sp):
            sp.dma_start(sc[:, 0, :], s1).then_inc(sc_loaded, 16)
            sp.dma_start(sc[:, 1, :], s2).then_inc(sc_loaded, 16)
            sp.dma_start(sc[:, 2, :], sh1).then_inc(sc_loaded, 16)
            sp.dma_start(sc[:, 3, :], sh2).then_inc(sc_loaded, 16)
            sp.dma_start(s3_sb[:], s3).then_inc(sc_loaded, 16)
            sp.dma_start(w12[0][:], w1.rearrange("(k p) n -> p k n", p=P)).then_inc(wf_loaded[0], 16)
            sp.dma_start(w12[1][:], w2.rearrange("(k p) n -> p k n", p=P)).then_inc(wf_loaded[1], 16)
            sp.dma_start(wh[0][:], wh1.rearrange("(k p) n -> p k n", p=P)).then_inc(wf_loaded[2], 16)
            sp.dma_start(wh[1][:], wh2.rearrange("(k p) n -> p k n", p=P)).then_inc(wf_loaded[3], 16)
            sp.dma_start(w3_sb[:], w3.rearrange("(k p) n -> p k n", p=P)).then_inc(wf_loaded[4], 16)

            def seq(b, u, i):
                sp.wait_ge(ln_chain, LN_STEPS * b + LN_STEPS)
                sp.dma_start(out_v[b], xf[u][:]).then_inc(stored, 16)

            pairs(sp, seq)
            sp.wait_ge(stored, 16 * NB)

        @block.gpsimd
        def _(pool):
            def seq(b, u, i):
                pool.wait_ge(stored, 32 * i)
                pool.dma_start(xf[u][:], x1_v[b]).then_inc(xf_loaded[u], 16)

            pairs(pool, seq)

        @block.tensor
        def _(pe):
            def begin(b, u, key):
                n = number[key]
                if n >= NBK:
                    pe.wait_ge(read[uses[n - NBK][1]], reader_count(b, uses[n - NBK][0]))
                elif not (isinstance(b, int) and b == 0):
                    k = n - NBK + NU
                    who = uses[k][1]
                    pe.wait_ge(read[who], per_seq[who] * b + (reads[k] - per_seq[who]))
                return bank_of(u, key)

            def seq(b, u, i):
                pe.wait_ge(xf_loaded[u], 16 * i + 16)
                for d in range(DT):
                    out_b = begin(b, u, ("xT", d))
                    for t in range(TT):
                        ins = nc.tensor.transpose(out_b[:, t * P:(t + 1) * P], xf[u][:, t, d * P:(d + 1) * P], ident[:])
                    ins.then_inc(filled, 1)

                def layer(name, m, w, k_tiles, x_in, source):
                    out_b = begin(b, u, (name, m))
                    for k in range(k_tiles):
                        if m == 0:
                            who = uses[number[source(k)]][1]
                            pe.wait_ge(read[who], reader_count(b, source(k)))
                        ins = nc.tensor.matmul(out_b, w[:, k, m * P:(m + 1) * P], x_in[:, k, :],
                                               start=k == 0, stop=k == k_tiles - 1)
                    ins.then_inc(filled, 1)

                for m in range(FT):
                    for j in range(2):
                        if m == 0:
                            pe.wait_ge(wf_loaded[j], 16)
                        layer(f"w{j + 1}", m, w12[j], DT, xT, lambda k: ("xT", k))
                for j, (x_in, source) in enumerate(((act_a, "w2"), (act_b, "h1"))):
                    pe.wait_ge(wf_loaded[2 + j], 16)
                    for m in range(FT):
                        layer(f"h{j + 1}", m, wh[j], FT, x_in, lambda k: (source, k))
                pe.wait_ge(wf_loaded[4], 16)
                for d in range(DT):
                    layer("w3", d, w3_sb, FT, act_a, lambda k: ("h2", k))
                for v in range(TT // 2):
                    out_b = begin(b, u, ("back", v))
                    for t in (2 * v, 2 * v + 1):
                        for d in range(DT):
                            pe.wait_ge(read["act"], reader_count(b, ("w3", d)))
                            ins = nc.tensor.transpose(out_b[:, (t % 2) * D + d * P:(t % 2) * D + (d + 1) * P],
                                                      yT[:, d, t * P:(t + 1) * P], ident[:])
                    ins.then_inc(filled, 1)

            pe.wait_ge(sc_loaded, 80)
            pairs(pe, seq)

        @block.scalar
        def _(act):
            act.wait_ge(sc_loaded, 80)

            def seq(b, u, i):
                def take(key):
                    act.wait_ge(filled, NU * b + (number[key] + 1))
                    return bank_of(u, key)

                for d in range(DT):
                    nc.scalar.activation(xT[:, d, :], take(("xT", d)), ACT.Copy).then_inc(read["act"], 1)
                for m in range(FT):
                    if m >= 2:
                        act.wait_ge(read["dve"], reader_count(b, ("w2", m - 2)))
                    nc.scalar.activation(gate[:, m % 2, :], take(("w1", m)), ACT.Silu,
                                         scale=sc[:, 0, m:m + 1]).then_inc(read["act"], 1)
                for name, dst, j in (("h1", act_b, 2), ("h2", act_a, 3)):
                    for m in range(FT):
                        nc.scalar.activation(dst[:, m, :], take((name, m)), ACT.Gelu,
                                             scale=sc[:, j, m:m + 1]).then_inc(read["act"], 1)
                for d in range(DT):
                    nc.scalar.activation(yT[:, d, :], take(("w3", d)), ACT.Copy,
                                         scale=s3_sb[:, d:d + 1]).then_inc(read["act"], 1)

            pairs(act, seq)

        @block.vector
        def _(dve):
            dve.wait_ge(sc_loaded, 80)

            def seq(b, u, i):
                for m in range(FT):
                    dve.wait_ge(filled, NU * b + (number[("w2", m)] + 1))
                    dve.wait_ge(read["act"], reader_count(b, ("w1", m)))
                    nc.vector.scalar_tensor_tensor(out=act_a[:, m, :], in0=bank_of(u, ("w2", m)),
                                                   scalar=sc[:, 1, m:m + 1], in1=gate[:, m % 2, :], op0=ALU.mult,
                                                   op1=ALU.mult).then_inc(read["dve"], 1)
                for v in range(TT // 2):
                    dve.wait_ge(filled, NU * b + (number[("back", v)] + 1))
                    rows = xf[u][:, 2 * v:2 * v + 2, :].rearrange("p t d -> p (t d)")
                    nc.vector.tensor_tensor(rows, rows, bank_of(u, ("back", v)), ALU.add).then_inc(read["dve"], 1)
                dve.wait_ge(read["dve"], reader_count(b, ("back", TT // 2 - 1)))
                layernorm(nc, dve, xf[u], xf[u], *ln_t, ln_chain, LN_STEPS * b)

            pairs(dve, seq)


def kernel(**inputs):
    import concourse.bacc as bacc
    from concourse.bass_utils import run_bass_kernel_spmd

    f32 = np.float32
    got = {k: np.asarray(v) for k, v in inputs.items()}
    A, B = "L0_attn_", "L0_ffn_"

    def even_odd(w):
        return w.reshape(NG, GH, DH // 2, 2, L).transpose(4, 0, 3, 1, 2).reshape(L, H * DH)

    inv_freq = 1.0 / 10000.0 ** (np.arange(0, DH, 2, dtype=f32) / DH)
    freqs = np.outer(np.arange(S, dtype=f32), inv_freq)
    twice = np.concatenate([freqs, freqs], -1)[:, ::2]
    rope = np.stack([np.tile(fn(twice).T, (GH, 1)) for fn in (np.cos, np.sin)], 1).astype(f32)

    def per_partition(v):
        return v.reshape(-1, P).T

    arrays = {
        "x": got[A + "x"],
        "w_dn": np.concatenate([got[A + "w_down_q"].T, got[A + "w_down_kv"].T], 1),
        "w_upq": even_odd(got[A + "w_up_q"]), "w_upk": even_odd(got[A + "w_up_k"]),
        "w_upv": got[A + "w_up_v"].T, "w_o": got[A + "w_out"].T,
        "ln_sb": np.stack([per_partition(got[A + "ln_scale"]), per_partition(got[A + "ln_bias"])], 1),
        "rope": rope,
        "w1": got[B + "w1_w"].T, "w2": got[B + "w2_w"].T, "wh1": got[B + "h1_w"].T, "wh2": got[B + "h2_w"].T,
        "w3": got[B + "w3_w"].T,
        "s1": per_partition(got[B + "w1_s"]), "s2": per_partition(got[B + "w2_s"]),
        "sh1": per_partition(got[B + "h1_s"]), "sh2": per_partition(got[B + "h2_s"]),
        "s3": per_partition(got[B + "w3_s"]),
    }
    arrays = {k: np.ascontiguousarray(v) for k, v in arrays.items()}
    nc = bacc.Bacc("TRN2", target_bir_lowering=False, num_devices=1)
    args = [nc.dram_tensor(k, v.shape, mybir.dt.from_np(v.dtype), kind="ExternalInput").ap() for k, v in arrays.items()]
    out = nc.dram_tensor("out", (NB, S, D), F32, kind="ExternalOutput").ap()
    build(nc, *args, out)
    return run_bass_kernel_spmd(nc, [arrays], core_ids=[0]).results[0]["out"]
```

```python
from contextlib import ExitStack

import numpy as np

import concourse.bass as bass
from concourse import mybir

F32 = mybir.dt.float32
F32R = mybir.dt.float32r
I32 = mybir.dt.int32
ACT = mybir.ActivationFunctionType
ALU = mybir.AluOpType
AX = mybir.AxisListType

P = 128
NB, S, D = 8, 512, 256
H, DH = 16, 64
L = 128
F = 1024
TT = S // P
DT = D // P
FT = F // P
NG, GH = 4, 4
HP = H // 2
EPS = 1e-5
RSQRT_MAGIC = 1597463007.0
NEWTON = 3
LN_STEPS = 2 * TT + 2 + 4 * NEWTON + TT

PROLOGUE = ([("hT", 0), ("hT", 1), ("c", 0), ("c", 1)] + [("v", t, 0) for t in range(TT)]
            + [("qk", w, e, g) for g in range(2) for w in range(2) for e in range(2)])
PER_SEQ = {"hT": DT, "c": 2, "v": 2 * TT, "qk": 4 * NG, "rb": HP, "ot": DT, "ob": TT // 2}


def nth(b, key):
    what = key[0]
    at = {"v": lambda t, half: TT * half + t, "qk": lambda w, e, g: 4 * g + 2 * w + e}.get(what, lambda i: i)(*key[1:])
    return PER_SEQ[what] * b + (at + 1)


def qk(w, g):
    return [("qk", w, 0, g), ("qk", w, 1, g)]


SCHED = [
    ([], [("rb", 7), ("ot", 0)], [("ot", 1)]),
    ([("ob", 0)], [("ob", 1)], []),
    (qk(0, 2), [("rb", 0)], []),
    (qk(1, 2), [], []),
    ([("rb", 1)], [("v", 0, 1)], [("v", 1, 1)]),
    ([], [("v", 2, 1)], [("v", 3, 1)]),
    (qk(0, 3), [("rb", 2)], []),
    (qk(1, 3), [("hT", 0)], [("hT", 1)]),
    ([("rb", 3)], [("c", 0)], [("c", 1)]),
    ([], [], []),
    (qk(0, 0), [("rb", 4)], []),
    (qk(1, 0), [("v", 0, 0)], []),
    ([("rb", 5)], [("v", 1, 0)], [("v", 2, 0)]),
    ([], [("v", 3, 0)], []),
    (qk(0, 1), [("rb", 6)], []),
    (qk(1, 1), [], []),
]
LN1_STEP, LN2_STEP = 5, 1
OF_PREV = [("rb", 7), ("ot", 0), ("ot", 1), ("ob", 0), ("ob", 1)]
OF_NEXT = PROLOGUE
LAST_USE = [key for places in SCHED for place in places for key in place][-1]

SLOTS = 2 * GH
QK_READS = 4


WF_AT, WF_COLS = [], 0
for _cols in (DT * F, DT * F, FT * F, FT * F, FT * D):
    WF_AT.append((WF_COLS, _cols))
    WF_COLS += _cols
LO_MASK = 0xFFF
CHECKS = 4
CHUNK = WF_COLS // (NB * CHECKS)
NBK, NWH = 4, 4
BACK = TT // 2


def build(nc, x, w_dn, w_upq, w_upk, w_upv, w_o, ln_sb, rope, wf, s1, s2, sh1, sh2, s3, out):
    x1_dram = nc.dram_tensor("x1_dram", (NB, P, TT * D), F32, kind="Internal").ap()
    ident_sem = nc.alloc_semaphore("ident_built")
    with ExitStack() as keep:
        ident = keep.enter_context(nc.sbuf_tensor("ident", [P, P], F32))
        low_bits = keep.enter_context(nc.sbuf_tensor("low_bits", [P, CHUNK], I32))
        attention(nc, x, w_dn, w_upq, w_upk, w_upv, w_o, ln_sb, rope, x1_dram, ident, ident_sem, wf, low_bits)
        ffn(nc, x1_dram, wf, s1, s2, sh1, sh2, s3, out, ident, low_bits)


def layernorm(nc, dve, rows, dst, stats, mv, ve, y, t, chain, base):
    n = [0]

    def link(ins, wait=True):
        n[0] += 1
        ins.then_inc(chain, 1)
        if wait:
            dve.wait_ge(chain, base + n[0])

    for i in range(TT):
        link(nc.vector.bn_stats(stats[:, i, :], rows[:, i, :]), wait=i == TT - 1)
    nc.vector.memset(t[:], 0.0)
    for i in range(TT):
        link(nc.vector.bn_aggr(mv[:, i, :], stats[:, i, :]), wait=i == TT - 1)
    link(nc.vector.tensor_scalar(ve[:], mv[:, :, 1], EPS, None, ALU.add))
    link(nc.vector.tensor_scalar(y[:].bitcast(I32), ve[:].bitcast(I32), -0.5, RSQRT_MAGIC, ALU.mult, ALU.add))
    for _ in range(NEWTON):
        link(nc.vector.tensor_tensor(t[:], y[:], y[:], ALU.mult))
        link(nc.vector.tensor_tensor(t[:], t[:], ve[:], ALU.mult))
        link(nc.vector.tensor_scalar(t[:], t[:], -0.5, 1.5, ALU.mult, ALU.add))
        link(nc.vector.tensor_tensor(y[:], y[:], t[:], ALU.mult))
    for i in range(TT):
        link(nc.vector.tensor_scalar(dst[:, i, :], rows[:, i, :], mv[:, i, 0:1], y[:, i:i + 1],
                                     ALU.subtract, ALU.mult), wait=False)
    assert n[0] == LN_STEPS


def attention(nc, x, w_dn, w_upq, w_upk, w_upv, w_o, ln_sb, rope, x1_dram, ident, ident_built, wf, low_bits):
    with ExitStack() as ctx:
        def sb(name, shape, dt=F32):
            return ctx.enter_context(nc.sbuf_tensor(name, shape, dt))

        def psum(name, shape):
            return ctx.enter_context(nc.psum_tensor(name, shape, F32))

        def sem(name):
            return ctx.enter_context(nc.semaphore(name))

        wdn = sb("wdn", [P, DT, 2 * L])
        wqk_hi = sb("wqk_hi", [P, 2, H * DH], F32R)
        wqk_lo = sb("wqk_lo", [P, 2, H * DH], F32R)
        wv_hi = sb("wv_hi", [P, H * DH], F32R)
        wv_lo = sb("wv_lo", [P, H * DH], F32R)
        wo = sb("wo", [P, HP, D])
        lnsb = sb("lnsb", [P, 2, DT])
        cs = sb("cs", [P, 2, S])
        xn = sb("xn", [P, TT, D])
        xr = sb("xr", [P, TT, D])
        c_hi = sb("c_hi", [P, 2, S], F32R)
        c_lo = sb("c_lo", [P, 2, S], F32R)
        rm = sb("rm", [P, 4, S])
        hl = sb("hl", [P, 2, 2, S], F32R)
        q_st = sb("q_st", [P, SLOTS, S], F32R)
        k_st = sb("k_st", [P, SLOTS, 2, S], F32R)
        v_st = sb("v_st", [P, TT, H, 2 * DH], F32R)
        ex = sb("ex", [P, 2, TT, S])
        pt_hi = sb("pt_hi", [P, 2, S], F32R)
        pt_lo = sb("pt_lo", [P, 2, S], F32R)
        ua = sb("ua", [P, S])
        ub = sb("ub", [P, S])
        at = sb("at", [P, HP, S])
        negmax = sb("negmax", [P, 2, TT])
        rsum = sb("rsum", [P, H, TT])
        rinv = sb("rinv", [P, H, TT])
        rinv_b = sb("rinv_b", [P, TT, 2, DH])
        ln_t = [sb(f"ln_{n}", s) for n, s in (("st", [P, TT, 6]), ("mv", [P, TT, 2]), ("ve", [P, TT]),
                                              ("y", [P, TT]), ("t", [P, TT]))]
        hT = sb("hT", [P, DT, S])
        chunk = sb("chunk", [P, CHUNK], I32)
        raw = at

        ps_s = psum("ps_s", [P, TT, S])
        ps_t = psum("ps_t", [P, 2, S])
        ps_v = psum("ps_v", [P, S])
        ps_m = psum("ps_m", [P, S])

        w_loaded = sem("w_loaded")
        up_loaded = [sem(f"up{i}_loaded") for i in range(3)]
        w_hi_done = sem("w_hi_done")
        w_lo_done = sem("w_lo_done")
        xn_loaded = sem("xn_loaded")
        xr_loaded = sem("xr_loaded")
        ln1_chain = sem("ln1_chain")
        ln2_chain = sem("ln2_chain")
        x1_stored = sem("x1_stored")
        ready = {what: sem(f"{what}_ready") for what in PER_SEQ}
        done = {what: sem(f"{what}_done") for what in PER_SEQ}
        c_hi_done = sem("c_hi_done")
        v_hi_done = sem("v_hi_done")
        rope_add = sem("rope_add")
        rope_hi = sem("rope_hi")
        rope_lo = sem("rope_lo")
        parked = sem("parked")
        placed = [[sem(f"placed_{n}{s}") for s in range(2)] for n in "qk"]
        s_ready = sem("s_ready")
        max_done = sem("max_done")
        exp_done = sem("exp_done")
        t_ready = sem("t_ready")
        pt_hi_done = sem("pt_hi_done")
        pt_lo_done = sem("pt_lo_done")
        pv_done = sem("pv_done")
        pv_copied = sem("pv_copied")
        u_summed = sem("u_summed")
        rinv_done = sem("rinv_done")
        rinv_b_done = sem("rinv_b_done")

        chunk_loaded = sem("chunk_loaded")
        chunk_seen = sem("chunk_seen")

        park = [[nc.dram_tensor(f"park_{n}{i}", (P, 4 * S), F32, kind="Internal").ap() for i in range(2)] for n in "qk"]
        x_v = x.rearrange("b (t p) d -> b p t d", p=P)
        wf_chunks = wf.rearrange("p (c n) -> c p n", n=CHUNK).bitcast(I32)
        x1_v = x1_dram.rearrange("b p (t d) -> b p t d", t=TT)

        def seqs(eng, body, prologue, epilogue):
            prologue()
            body(0, first=True)
            with eng.Fori(1, NB - 1) as b:
                body(b)
            body(NB - 1, last=True)
            epilogue()

        def keys(h, place, first, last):
            for key in SCHED[h][place]:
                of = -1 if key in OF_PREV else 1 if key in OF_NEXT else 0
                if not (first and of < 0) and not (last and of > 0):
                    yield key, of

        block = ctx.enter_context(nc.Block())

        @block.sync
        def _(sp):
            def moves(b, w, g):
                sp.wait_ge(rope_lo, 2 * NG * b + (2 * g + w + 1))
                spot = park[w][g % 2]
                sp.dma_start(spot, hl[:].rearrange("p e a s -> p (e a s)").bitcast(F32)).then_inc(parked, 16)
                sp.wait_ge(parked, 32 * NG * b + 16 * (2 * g + w + 1))
                s0 = GH * (g % 2)
                blocks = spot.rearrange("(j r) (e a s) -> a e r j s", j=GH, a=2, e=2)
                both = spot.rearrange("(j r) (e z) -> e r j z", j=GH, e=2)
                for half in range(2):
                    for e in range(2):
                        r0 = 64 * half + 32 * e
                        if w == 0:
                            sp.dma_start(q_st[r0:r0 + 32, s0:s0 + GH, :].bitcast(F32),
                                         blocks[half, e]).then_inc(placed[w][g % 2], 16)
                        else:
                            sp.dma_start(k_st[r0:r0 + 32, s0:s0 + GH].rearrange("r j a s -> r j (a s)").bitcast(F32),
                                         both[e]).then_inc(placed[w][g % 2], 16)

            def load_xn(b):
                sp.dma_start(xn[:], x_v[b]).then_inc(xn_loaded, 16)

            def load_xr(b):
                sp.dma_start(xr[:], x_v[b]).then_inc(xr_loaded, 16)

            def prologue():
                sp.dma_start(xn[:], x_v[0]).then_inc(xn_loaded, 16)
                sp.dma_start(lnsb[:], ln_sb).then_inc(w_loaded, 16)
                sp.dma_start(wdn[:], w_dn.rearrange("(k p) n -> p k n", p=P)).then_inc(w_loaded, 16)
                for i, w in enumerate((w_upq, w_upk, w_upv)):
                    sp.dma_start(raw[:, 2 * i:2 * i + 2, :], w.rearrange("p (a s) -> p a s", s=S)).then_inc(up_loaded[i], 16)
                sp.dma_start(cs[:], rope).then_inc(w_loaded, 16)
                sp.dma_start(wo[:], w_o.rearrange("(k p) n -> p k n", p=P)).then_inc(w_loaded, 16)
                load_xr(0)
                sp.wait_ge(done["hT"], DT)
                load_xn(1)
                for g in range(2):
                    for w in range(2):
                        moves(0, w, g)

            def store_x1(b):
                sp.wait_ge(ln2_chain, LN_STEPS * (b + 1))
                sp.dma_start(x1_v[b], xr[:]).then_inc(x1_stored, 16)

            def body(b, first=False, last=False):
                for h in range(H):
                    if h % (H // CHECKS) == 2:
                        i = h // (H // CHECKS)
                        sp.wait_ge(chunk_seen, CHECKS * b + (i + 1))
                        sp.dma_start(chunk[:], wf_chunks[CHECKS * b + i]).then_inc(chunk_loaded, 16)
                    if h == 0 and not last and not first:
                        sp.wait_ge(done["hT"], DT * b + DT)
                        load_xn(b + 1)
                    if h == 2 and not first:
                        store_x1(b - 1)
                    if h == 3 and not first:
                        sp.wait_ge(x1_stored, 16 * b)
                        load_xr(b)
                    for place in range(3):
                        for key, of in keys(h, place, first, last):
                            if key[0] == "qk" and key[2] == 1:
                                moves(b + of, key[1], key[3])

            def epilogue():
                store_x1(NB - 1)
                sp.wait_ge(x1_stored, 16 * NB)

            seqs(sp, body, prologue, epilogue)

        @block.tensor
        def _(pe):
            before = [None]

            def misc(b, key):
                if before[0]:
                    pe.wait_ge(done[before[0][1][0]], nth(*before[0]))
                before[0] = (b, key)
                what = key[0]
                if what == "hT":
                    pe.wait_ge(ln1_chain, LN_STEPS * (b + 1))
                    for t in range(TT):
                        ins = nc.tensor.transpose(ps_m[:, t * P:(t + 1) * P], xn[:, t, key[1] * P:(key[1] + 1) * P], ident[:])
                elif what == "c":
                    pe.wait_ge(done["hT"], DT * b + DT)
                    for k in range(DT):
                        ins = nc.tensor.matmul(ps_m[:], wdn[:, k, key[1] * L:(key[1] + 1) * L], hT[:, k, :],
                                               start=k == 0, stop=k == DT - 1)
                elif what == "v":
                    pe.wait_ge(done["c"], 2 * b + 2)
                    t, half = key[1], key[2]
                    lhs = (c_hi, c_hi, c_lo)
                    rhs = (wv_hi, wv_lo, wv_hi)
                    for i in range(3):
                        ins = nc.tensor.matmul(ps_m[:], lhs[i][:, 1, t * P:(t + 1) * P],
                                               rhs[i][:, half * S:(half + 1) * S], start=i == 0, stop=i == 2)
                elif what == "qk":
                    pe.wait_ge(done["c"], 2 * b + 2)
                    w, e, g = key[1:]
                    col = (2 * g + e) * P
                    lhs = (wqk_hi, wqk_lo, wqk_hi)
                    rhs = (c_hi, c_hi, c_lo)
                    for i in range(3):
                        ins = nc.tensor.matmul(ps_m[:], lhs[i][:, w, col:col + P], rhs[i][:, w, :],
                                               start=i == 0, stop=i == 2)
                elif what == "rb":
                    p = key[1]
                    pe.wait_ge(rinv_b_done, HP * b + p + 1)
                    for t in range(TT):
                        ins = nc.tensor.transpose(ps_m[:, t * P:(t + 1) * P],
                                                  rinv_b[:, t].rearrange("p h d -> p (h d)"), ident[:])
                elif what == "ot":
                    pe.wait_ge(done["rb"], HP * b + HP)
                    for p in range(HP):
                        ins = nc.tensor.matmul(ps_m[:], wo[:, p, key[1] * P:(key[1] + 1) * P], at[:, p, :],
                                               start=p == 0, stop=p == HP - 1)
                elif what == "ob":
                    pe.wait_ge(done["ot"], DT * b + DT)
                    for i in range(2):
                        t = 2 * key[1] + i
                        for d in range(DT):
                            ins = nc.tensor.transpose(ps_m[:, i * D + d * P:i * D + (d + 1) * P],
                                                      hT[:, d, t * P:(t + 1) * P], ident[:])
                ins.then_inc(ready[what], 1)

            def scores(b, h, pair):
                slot, g = h % SLOTS, h // GH
                if pair == 0 and h % GH == 0:
                    for w in range(2):
                        pe.wait_ge(placed[w][g % 2], 16 * QK_READS * (NG // 2 * b + (g // 2 + 1)))
                if h > 0:
                    pe.wait_ge(exp_done, TT * H * b + TT * (h - 1) + 2 * pair + 2)
                elif not (isinstance(b, int) and b == 0):
                    pe.wait_ge(exp_done, TT * H * b + (2 * pair - 2))
                for i in range(2):
                    t = 2 * pair + i
                    for part in range(2):
                        ins = nc.tensor.matmul(ps_s[:, t, :], q_st[:, slot, t * P:(t + 1) * P], k_st[:, slot, part, :],
                                               start=part == 0, stop=part == 1)
                ins.then_inc(s_ready, 1)

            def transposes(b, h, kt):
                n = TT * h + kt
                if kt == 0:
                    pe.wait_ge(exp_done, TT * H * b + TT * (h + 1))
                if n >= 2:
                    pe.wait_ge(pt_lo_done, TT * H * b + n - 1)
                for t in range(TT):
                    ins = nc.tensor.transpose(ps_t[:, kt % 2, t * P:(t + 1) * P], ex[:, h % 2, t, kt * P:(kt + 1) * P], ident[:])
                ins.then_inc(t_ready, 1)

            def values(b, h, kt):
                if kt == 0:
                    pe.wait_ge(pv_copied, H * b + h)
                    if h == 0:
                        pe.wait_ge(done["v"], 2 * TT * b + TT)
                    if h == H // 2:
                        pe.wait_ge(done["v"], 2 * TT * b + 2 * TT)
                pe.wait_ge(pt_lo_done, TT * H * b + TT * h + kt + 1)
                nc.tensor.matmul(ps_v[:], v_st[:, kt, h, :], pt_hi[:, kt % 2, :], start=kt == 0, stop=False)
                nc.tensor.matmul(ps_v[:], v_st[:, kt, h, :], pt_lo[:, kt % 2, :], start=False,
                                 stop=kt == TT - 1).then_inc(pv_done, 1)

            def prologue():
                pe.wait_ge(ident_built, 2)
                pe.wait_ge(w_loaded, 64)
                pe.wait_ge(w_lo_done, 3)
                for key in PROLOGUE:
                    misc(0, key)
                scores(0, 0, 0)
                scores(0, 0, 1)

            def body(b, first=False, last=False):
                if not first:
                    before[0] = (b, LAST_USE)

                def place(h, i):
                    for key, of in keys(h, i, first, last):
                        misc(b + of, key)

                def next_scores(h, pair):
                    if h + 1 < H:
                        scores(b, h + 1, pair)
                    elif not last:
                        scores(b + 1, 0, pair)

                for h in range(H):
                    next_scores(h, 0)
                    transposes(b, h, 0)
                    transposes(b, h, 1)
                    place(h, 0)
                    next_scores(h, 1)
                    values(b, h, 0)
                    transposes(b, h, 2)
                    place(h, 1)
                    values(b, h, 1)
                    transposes(b, h, 3)
                    values(b, h, 2)
                    place(h, 2)
                    values(b, h, 3)

            def epilogue():
                for key in OF_PREV:
                    misc(NB - 1, key)

            seqs(pe, body, prologue, epilogue)

        @block.scalar
        def _(act):
            def exps(b, h, pair):
                act.wait_ge(max_done, 2 * H * b + (2 * h + pair + 1))
                for t in (2 * pair, 2 * pair + 1):
                    nc.scalar.activation(ex[:, h % 2, t, :], ps_s[:, t, :], ACT.Exp, bias=negmax[:, h % 2, t:t + 1],
                                         accum_out=rsum[:, h, t:t + 1]).then_inc(exp_done, 1)

            def pt_his(b, h, kt):
                n = TT * h + kt
                act.wait_ge(t_ready, TT * H * b + (n + 1))
                if n >= 2:
                    act.wait_ge(pv_done, TT * H * b + (n - 1))
                nc.scalar.activation(pt_hi[:, kt % 2, :], ps_t[:, kt % 2, :], ACT.Copy).then_inc(pt_hi_done, 1)

            def copy_pv(b, h):
                act.wait_ge(pv_done, TT * H * b + (TT * h + TT))
                act.wait_ge(done["rb"], HP * b + h // 2)
                r = DH * (h % 2)
                nc.scalar.activation(ua[r:r + DH, :], ps_v[0:DH, :], ACT.Copy)
                nc.scalar.activation(ub[r:r + DH, :], ps_v[DH:2 * DH, :], ACT.Copy).then_inc(pv_copied, 1)

            def rope_his(b, w, g):
                act.wait_ge(rope_add, 2 * NG * b + (2 * g + w + 1))
                act.wait_ge(parked, 32 * NG * b + 16 * (2 * g + w))
                nc.scalar.activation(hl[:, :, 0, :], rm[:, 0:2, :], ACT.Copy).then_inc(rope_hi, 1)

            def misc(b, key):
                what = key[0]
                if what in ("c", "v", "ot"):
                    act.wait_ge(ready[what], nth(b, key))
                if what == "c":
                    nc.scalar.activation(c_hi[:, key[1], :], ps_m[:], ACT.Copy).then_inc(c_hi_done, 1)
                elif what == "v":
                    t, half = key[1:]
                    nc.scalar.activation(v_st[:, t, half * (H // 2):(half + 1) * (H // 2), 0:DH],
                                         ps_m[:].rearrange("p (h d) -> p h d", d=DH), ACT.Copy).then_inc(v_hi_done, 1)
                elif what == "ot":
                    nc.scalar.activation(hT[:, key[1], :], ps_m[:], ACT.Copy).then_inc(done["ot"], 1)

            def prologue():
                for key in PROLOGUE:
                    misc(0, key)
                    if key[0] == "qk" and key[2] == 1:
                        rope_his(0, key[1], key[3])
                exps(0, 0, 0)
                exps(0, 0, 1)

            def body(b, first=False, last=False):
                def place(h, i):
                    for key, of in keys(h, i, first, last):
                        misc(b + of, key)

                def next_exps(h, pair):
                    if h + 1 < H:
                        exps(b, h + 1, pair)
                    elif not last:
                        exps(b + 1, 0, pair)

                for h in range(H):
                    if h > 0:
                        copy_pv(b, h - 1)
                    elif not first:
                        copy_pv(b - 1, H - 1)
                    pt_his(b, h, 0)
                    pt_his(b, h, 1)
                    place(h, 0)
                    next_exps(h, 0)
                    pt_his(b, h, 2)
                    place(h, 1)
                    pt_his(b, h, 3)
                    next_exps(h, 1)
                    place(h, 2)
                    for i in range(3):
                        for key, of in keys(h, i, first, last):
                            if key[0] == "qk" and key[2] == 1:
                                rope_his(b + of, key[1], key[3])

            def epilogue():
                copy_pv(NB - 1, H - 1)
                for key in OF_PREV:
                    misc(NB - 1, key)

            seqs(act, body, prologue, epilogue)

        @block.vector
        def _(dve):
            def maxes(b, h, pair):
                dve.wait_ge(s_ready, 2 * H * b + (2 * h + pair + 1))
                nc.vector.tensor_reduce(negmax[:, h % 2, 2 * pair:2 * pair + 2], ps_s[:, 2 * pair:2 * pair + 2, :],
                                        AX.X, ALU.max, negate=True).then_inc(max_done, 1)

            def pt_los(b, h, kt):
                dve.wait_ge(pt_hi_done, TT * H * b + (TT * h + kt + 1))
                nc.vector.tensor_tensor(pt_lo[:, kt % 2, :], ps_t[:, kt % 2, :], pt_hi[:, kt % 2, :].bitcast(F32),
                                        ALU.subtract).then_inc(pt_lo_done, 1)

            def rinvs(b, p):
                dve.wait_ge(exp_done, TT * H * b + TT * 2 * (p + 1))
                r = rinv[:, 2 * p:2 * p + 2, :]
                nc.vector.reciprocal(r, rsum[:, 2 * p:2 * p + 2, :]).then_inc(rinv_done, 1)
                dve.wait_ge(rinv_done, HP * b + (p + 1))
                nc.vector.tensor_copy(rinv_b[:], r.rearrange("p h t -> p t h").unsqueeze(3).broadcast_to([P, TT, 2, DH])
                                      ).then_inc(rinv_b_done, 1)

            def misc(b, key):
                what = key[0]
                if what != "ot":
                    dve.wait_ge(ready[what], nth(b, key))
                if what == "hT":
                    d = key[1]
                    nc.vector.tensor_scalar(hT[:, d, :], ps_m[:], lnsb[:, 0, d:d + 1], lnsb[:, 1, d:d + 1],
                                            ALU.mult, ALU.add).then_inc(done["hT"], 1)
                elif what == "c":
                    dve.wait_ge(c_hi_done, 2 * b + (key[1] + 1))
                    nc.vector.tensor_tensor(c_lo[:, key[1], :], ps_m[:], c_hi[:, key[1], :].bitcast(F32),
                                            ALU.subtract).then_inc(done["c"], 1)
                elif what == "v":
                    t, half = key[1:]
                    dve.wait_ge(v_hi_done, nth(b, key))
                    heads = slice_of(half)
                    nc.vector.tensor_tensor(v_st[:, t, heads[0]:heads[1], DH:2 * DH],
                                            ps_m[:].rearrange("p (h d) -> p h d", d=DH),
                                            v_st[:, t, heads[0]:heads[1], 0:DH].bitcast(F32),
                                            ALU.subtract).then_inc(done["v"], 1)
                elif what == "qk":
                    w, e, g = key[1:]
                    if e == 0:
                        dve.wait_ge(rope_lo, 2 * NG * b + (2 * g + w))
                        a0, a1 = (0, 0), (1, 1)
                    else:
                        a0, a1 = (2, 1), (3, 0)
                    nc.vector.tensor_tensor(rm[:, a0[0], :], ps_m[:], cs[:, a0[1], :], ALU.mult)
                    nc.vector.tensor_tensor(rm[:, a1[0], :], ps_m[:], cs[:, a1[1], :], ALU.mult).then_inc(done["qk"], 1)
                elif what == "rb":
                    p = key[1]
                    dve.wait_ge(u_summed, HP * b + (p + 1))
                    nc.vector.tensor_tensor(at[:, p, :], ps_m[:], ua[:], ALU.mult).then_inc(done["rb"], 1)
                elif what == "ob":
                    u = key[1]
                    dve.wait_ge(xr_loaded, 16 * b + 16)
                    v = xr[:, 2 * u:2 * u + 2, :].rearrange("p t d -> p (t d)")
                    nc.vector.scalar_tensor_tensor(out=v, in0=v, scalar=2.0, in1=ps_m[:], op0=ALU.mult,
                                                   op1=ALU.add).then_inc(done["ob"], 1)

            def ln1(b):
                dve.wait_ge(xn_loaded, 16 * b + 16)
                layernorm(nc, dve, xn, xn, *ln_t, ln1_chain, LN_STEPS * b)

            def ln2(b):
                dve.wait_ge(done["ob"], 2 * b + 2)
                layernorm(nc, dve, xr, xr, *ln_t, ln2_chain, LN_STEPS * b)

            def prologue():
                for i, (hi, lo, scale) in enumerate(((wqk_hi[:, 0], wqk_lo[:, 0], DH ** -0.5),
                                                     (wqk_hi[:, 1], wqk_lo[:, 1], 1.0), (wv_hi[:], wv_lo[:], 1.0))):
                    dve.wait_ge(up_loaded[i], 16)
                    r = raw[:, 2 * i:2 * i + 2, :].rearrange("p a s -> p (a s)")
                    nc.vector.tensor_scalar(hi, r, scale, None, ALU.mult).then_inc(w_hi_done, 1)
                    dve.wait_ge(w_hi_done, i + 1)
                    nc.vector.scalar_tensor_tensor(out=lo, in0=r, scalar=scale, in1=hi.bitcast(F32), op0=ALU.mult,
                                                   op1=ALU.subtract).then_inc(w_lo_done, 1)
                ln1(0)
                dve.wait_ge(w_loaded, 64)
                for key in PROLOGUE:
                    misc(0, key)
                maxes(0, 0, 0)
                maxes(0, 0, 1)

            def body(b, first=False, last=False):
                def place(h, i):
                    for key, of in keys(h, i, first, last):
                        misc(b + of, key)

                def next_maxes(h, pair):
                    if h + 1 < H:
                        maxes(b, h + 1, pair)
                    elif not last:
                        maxes(b + 1, 0, pair)

                for h in range(H):
                    if h % (H // CHECKS) == (H // CHECKS) - 1:
                        n = h // (H // CHECKS)
                        dve.wait_ge(chunk_loaded, 16 * CHECKS * b + 16 * (n + 1))
                        dve.wait_ge(chunk_seen, CHECKS * b + (n + 1))
                        nc.vector.tensor_tensor(low_bits[:], low_bits[:], chunk[:], ALU.bitwise_or).then_inc(chunk_seen, 1)
                    next_maxes(h, 0)
                    pt_los(b, h, 0)
                    pt_los(b, h, 1)
                    if h % 2 == 1:
                        rinvs(b, h // 2)
                    place(h, 0)
                    next_maxes(h, 1)
                    pt_los(b, h, 2)
                    place(h, 1)
                    pt_los(b, h, 3)
                    place(h, 2)
                    if h == LN2_STEP and not first:
                        ln2(b - 1)
                    if h == LN1_STEP and not last:
                        ln1(b + 1)

            def epilogue():
                for key in OF_PREV:
                    misc(NB - 1, key)
                ln2(NB - 1)

            seqs(dve, body, prologue, epilogue)

        @block.gpsimd
        def _(pool):
            def add_parts(b, p):
                pool.wait_ge(pv_copied, H * b + (2 * p + 2))
                nc.gpsimd.tensor_tensor(ua[:], ua[:], ub[:], ALU.add).then_inc(u_summed, 1)

            def rotate(b, w, g):
                pool.wait_ge(done["qk"], nth(b, ("qk", w, 1, g)))
                nc.gpsimd.tensor_tensor(rm[:, 0, :], rm[:, 0, :], rm[:, 2, :], ALU.subtract)
                nc.gpsimd.tensor_tensor(rm[:, 1, :], rm[:, 1, :], rm[:, 3, :], ALU.add).then_inc(rope_add, 1)
                pool.wait_ge(rope_hi, 2 * NG * b + (2 * g + w + 1))
                nc.gpsimd.tensor_tensor(hl[:, :, 1, :], rm[:, 0:2, :], hl[:, :, 0, :].bitcast(F32),
                                        ALU.subtract).then_inc(rope_lo, 1)

            def prologue():
                nc.gpsimd.memset(ident[:], 0.0).then_inc(ident_built, 1)
                pool.wait_ge(ident_built, 1)
                nc.gpsimd.affine_select(out=ident[:], in_=ident[:], compare_op=ALU.not_equal, fill=1.0, base=0,
                                        pattern=[[-1, P]], channel_multiplier=1).then_inc(ident_built, 1)
                nc.gpsimd.memset(low_bits[:], 0).then_inc(chunk_seen, 1)
                for g in range(2):
                    for w in range(2):
                        rotate(0, w, g)

            def body(b, first=False, last=False):
                for h in range(H):
                    if h % 2 == 0 and h > 0:
                        add_parts(b, h // 2 - 1)
                    elif h == 0 and not first:
                        add_parts(b - 1, HP - 1)
                    for i in range(3):
                        for key, of in keys(h, i, first, last):
                            if key[0] == "qk" and key[2] == 1:
                                rotate(b + of, key[1], key[3])

            def epilogue():
                add_parts(NB - 1, HP - 1)

            seqs(pool, body, prologue, epilogue)


def slice_of(half):
    return half * (H // 2), (half + 1) * (H // 2)


def ffn(nc, x1_dram, wf, s1, s2, sh1, sh2, s3, out, ident, low_bits):
    with ExitStack() as ctx:
        def sb(name, shape, dt=F32):
            return ctx.enter_context(nc.sbuf_tensor(name, shape, dt))

        def sem(name):
            return ctx.enter_context(nc.semaphore(name))

        with nc.sbuf_tensor("w_f32", [P, WF_COLS], F32) as w_f32:
            pass
        w_r = sb("w_r", [P, WF_COLS], F32R)
        sc = sb("sc", [P, 4, FT])
        s3_sb = sb("s3_sb", [P, DT])
        xf = [sb(f"xf{i}", [P, TT, D]) for i in range(2)]
        xT = sb("xT", [P, DT, 2, S], F32R)
        act_a = sb("act_a", [P, FT, 2, S], F32R)
        act_b = sb("act_b", [P, FT, 2, S], F32R)
        gate = sb("gate", [P, 2, S])
        whole = sb("whole", [P, NWH, S])
        yT = sb("yT", [P, DT, S])
        low = sb("low", [P, 1])
        general = sb("general", [1, 1], I32)
        ln_t = [sb(f"lnf_{n}", s) for n, s in (("st", [P, TT, 6]), ("mv", [P, TT, 2]), ("ve", [P, TT]),
                                               ("y", [P, TT]), ("t", [P, TT]))]
        bank = ctx.enter_context(nc.psum_tensor("bank", [P, NBK, S], F32))
        bank_y = ctx.enter_context(nc.psum_tensor("bank_y", [P, DT, S], F32))
        bank_x = ctx.enter_context(nc.psum_tensor("bank_x", [P, 2, S], F32))

        w_loaded = [sem(f"wf{i}_loaded") for i in range(len(WF_AT))]
        w_rounded = [sem(f"wf{i}_rounded") for i in range(len(WF_AT))]
        w_again = sem("w_again")
        sc_loaded = sem("sc_loaded")
        xf_loaded = [sem(f"xf{i}_loaded") for i in range(2)]
        stored = sem("stored")
        flag_steps = sem("flag_steps")
        flag_across = sem("flag_across")
        filled = sem("filled")
        gate_done = sem("gate_done")
        gated = sem("gated")
        gelu_done = sem("gelu_done")
        hi_done = sem("hi_done")
        lo_done = sem("lo_done")
        x_turned = sem("x_turned")
        xT_hi = sem("xT_hi")
        xT_lo = sem("xT_lo")
        y_ready = sem("y_ready")
        y_copied = sem("y_copied")
        y_turned = sem("y_turned")
        y_added = sem("y_added")
        ln_chain = sem("lnf_chain")

        x1_v = x1_dram.rearrange("b p (t d) -> b p t d", t=TT)
        out_v = out.rearrange("b (t p) d -> b p t d", p=P)
        block = ctx.enter_context(nc.Block())

        def seqs(eng, seq):
            seq(0, 0, 1, first=True)
            with eng.Fori(0, NB // 2 - 1) as i:
                seq(2 * i + 1, 1, i + 2)
                seq(2 * i + 2, 0, i + 2)
            seq(NB - 1, 1, None, last=True)

        @block.sync
        def _(sp):
            for i, s in enumerate((s1, s2, sh1, sh2)):
                sp.dma_start(sc[:, i, :], s).then_inc(sc_loaded, 16)
            sp.dma_start(s3_sb[:], s3).then_inc(sc_loaded, 16)
            sp.dma_start(xf[0][:], x1_v[0]).then_inc(xf_loaded[0], 16)
            for i, (at, cols) in enumerate(WF_AT):
                sp.dma_start(w_f32[:, at:at + cols], wf[:, at:at + cols]).then_inc(w_loaded[i], 16)
            sp.dma_start(xf[1][:], x1_v[1]).then_inc(xf_loaded[1], 16)

            def store(b, u):
                sp.wait_ge(ln_chain, LN_STEPS * b + LN_STEPS)
                sp.dma_start(out_v[b], xf[u][:]).then_inc(stored, 16)

            def seq(b, u, load, first=False, last=False):
                if not first:
                    store(b - 1, 1 - u)
                    if not last:
                        sp.wait_ge(stored, 16 * b)
                        sp.dma_start(xf[1 - u][:], x1_v[b + 1]).then_inc(xf_loaded[1 - u], 16)

            seqs(sp, seq)
            store(NB - 1, 1)
            sp.wait_ge(stored, 16 * NB)

        @block.tensor
        def _(pe):
            def x_in(u, load):
                pe.wait_ge(xf_loaded[u], 16 * load)
                for d in range(DT):
                    for t in range(TT):
                        ins = nc.tensor.transpose(bank_x[:, d, t * P:(t + 1) * P], xf[u][:, t, d * P:(d + 1) * P],
                                                  ident[:])
                    ins.then_inc(x_turned, 1)

            def back(b):
                for v in range(BACK):
                    for t in (2 * v, 2 * v + 1):
                        for d in range(DT):
                            if t == 0:
                                pe.wait_ge(y_copied, DT * b + d + 1)
                            ins = nc.tensor.transpose(bank_x[:, v, (t % 2) * D + d * P:(t % 2) * D + (d + 1) * P],
                                                      yT[:, d, t * P:(t + 1) * P], ident[:])
                    ins.then_inc(y_turned, 1)

            def network(dt):
                def weights(i, m, k, width):
                    at = WF_AT[i][0] + k * width + m * P
                    return (w_r if dt == F32R else w_f32)[:, at:at + P]

                def product(dst, w, x, k, k_tiles):
                    for part in range(2):
                        xp = x[:, k, part, :] if dt == F32R else x[:, k, part, :].bitcast(F32)
                        ins = nc.tensor.matmul(dst, w, xp, start=k + part == 0, stop=k + part == k_tiles)
                    return ins

                def begin(b, n, first):
                    m = n - NBK
                    if m < 0:
                        if not first:
                            pe.wait_ge(gelu_done, 2 * FT * b + (m + 1))
                    elif m < 2 * FT:
                        pe.wait_ge((gate_done, gated)[m % 2], FT * b + (m // 2 + 1))
                    else:
                        pe.wait_ge(gelu_done, 2 * FT * b + (m - 2 * FT + 1))
                    return bank[:, n % NBK, :]

                def seq(b, u, load, first=False, last=False):
                    for m in range(FT):
                        for j in range(2):
                            if first and m == 0:
                                pe.wait_ge(w_rounded[j], 1)
                            dst = begin(b, 2 * m + j, first)
                            for k in range(DT):
                                if m == 0 and j == 0:
                                    pe.wait_ge(xT_lo, DT * b + (k + 1))
                                ins = product(dst, weights(j, m, k, F), xT, k, DT)
                            ins.then_inc(filled, 1)
                        if m == 1 and not first:
                            back(b - 1)
                    for j, source in enumerate((act_a, act_b)):
                        if first:
                            pe.wait_ge(w_rounded[2 + j], 1)
                        for ms in [(0, 1)] + [(m,) for m in range(2, FT)]:
                            dsts = [begin(b, 2 * FT + FT * j + m, first) for m in ms]
                            for k in range(FT):
                                if ms[0] == 0:
                                    pe.wait_ge(lo_done, 3 * FT * b + (FT * j + k + 1))
                                for m, dst in zip(ms, dsts):
                                    ins = product(dst, weights(2 + j, m, k, F), source, k, FT)
                                    if k == FT - 1:
                                        ins.then_inc(filled, 1)
                    if not last:
                        if not first:
                            pe.wait_ge(y_added, BACK * b)
                        x_in(1 - u, load)
                    if first:
                        pe.wait_ge(w_rounded[4], 1)
                    for k in range(FT):
                        pe.wait_ge(lo_done, 3 * FT * b + (2 * FT + k + 1))
                        for d in range(DT):
                            ins = product(bank_y[:, d, :], weights(4, d, k, D), act_a, k, FT)
                            if k == FT - 1:
                                ins.then_inc(y_ready, 1)

                seqs(pe, seq)

            pe.wait_ge(flag_steps, 2)
            nc.tensor.transpose(bank_x[0:1, 0, 0:P], low[:], ident[:]).then_inc(flag_across, 1)
            pe.wait_ge(flag_steps, 4)
            x_in(0, 1)
            flag = pe.value_load(general[0:1, 0:1], min_val=0, max_val=1)
            with pe.If(flag < 1):
                network(F32R)
            with pe.If(flag > 0):
                pe.wait_ge(w_again, 16)
                network(F32)
            back(NB - 1)

        @block.gpsimd
        def _(pool):
            pool.wait_ge(flag_steps, 4)
            flag = pool.value_load(general[0:1, 0:1], min_val=0, max_val=1)
            with pool.If(flag > 0):
                for i in range(len(WF_AT)):
                    pool.wait_ge(w_rounded[i], 1)
                pool.dma_start(w_f32[:], wf).then_inc(w_again, 16)

        @block.scalar
        def _(act):
            def x_parts(b):
                for d in range(DT):
                    act.wait_ge(x_turned, DT * b + (d + 1))
                    nc.scalar.activation(xT[:, d, 0, :], bank_x[:, d, :], ACT.Copy).then_inc(xT_hi, 1)

            def hi(b, n, dst):
                nc.scalar.activation(dst[:, n % FT, 0, :], whole[:, n % NWH, :], ACT.Copy).then_inc(hi_done, 1)

            def seq(b, u, load, first=False, last=False):
                for m in range(FT + 1):
                    if m < FT:
                        act.wait_ge(filled, 4 * FT * b + (2 * m + 1))
                        if m >= 2:
                            act.wait_ge(gated, FT * b + (m - 1))
                        nc.scalar.activation(gate[:, m % 2, :], bank[:, 2 * m % NBK, :], ACT.Silu,
                                             scale=sc[:, 0, m:m + 1]).then_inc(gate_done, 1)
                    if m > 0:
                        act.wait_ge(gated, FT * b + m)
                        hi(b, m - 1, act_a)
                for j, dst in enumerate((act_b, act_a)):
                    for m in range(FT):
                        n = FT + FT * j + m
                        act.wait_ge(filled, 4 * FT * b + (FT + n + 1))
                        act.wait_ge(lo_done, 3 * FT * b + (n - NWH + 1))
                        nc.scalar.activation(whole[:, n % NWH, :], bank[:, (FT + n) % NBK, :], ACT.Gelu,
                                             scale=sc[:, 2 + j, m:m + 1]).then_inc(gelu_done, 1)
                        act.wait_ge(gelu_done, 2 * FT * b + (n - FT + 1))
                        hi(b, n, dst)
                if not last:
                    x_parts(b + 1)
                for d in range(DT):
                    act.wait_ge(y_ready, DT * b + (d + 1))
                    nc.scalar.activation(yT[:, d, :], bank_y[:, d, :], ACT.Copy,
                                         scale=s3_sb[:, d:d + 1]).then_inc(y_copied, 1)

            act.wait_ge(sc_loaded, 80)
            x_parts(0)
            for i in (2, 4):
                act.wait_ge(w_loaded[i], 16)
                at, cols = WF_AT[i]
                nc.scalar.activation(w_r[:, at:at + cols], w_f32[:, at:at + cols], ACT.Copy).then_inc(w_rounded[i], 1)
            seqs(act, seq)

        @block.vector
        def _(dve):
            def x_parts(b):
                for d in range(DT):
                    dve.wait_ge(xT_hi, DT * b + (d + 1))
                    nc.vector.tensor_tensor(xT[:, d, 1, :], bank_x[:, d, :], xT[:, d, 0, :].bitcast(F32),
                                            ALU.subtract).then_inc(xT_lo, 1)

            def lo(b, n, dst):
                dve.wait_ge(hi_done, 3 * FT * b + (n + 1))
                nc.vector.tensor_tensor(dst[:, n % FT, 1, :], whole[:, n % NWH, :], dst[:, n % FT, 0, :].bitcast(F32),
                                        ALU.subtract).then_inc(lo_done, 1)

            def finish(b, u):
                for v in range(BACK):
                    dve.wait_ge(y_turned, BACK * b + (v + 1))
                    rows = xf[u][:, 2 * v:2 * v + 2, :].rearrange("p t d -> p (t d)")
                    nc.vector.tensor_tensor(rows, rows, bank_x[:, v, :], ALU.add).then_inc(y_added, 1)
                dve.wait_ge(y_added, BACK * b + BACK)
                layernorm(nc, dve, xf[u], xf[u], *ln_t, ln_chain, LN_STEPS * b)

            def seq(b, u, load, first=False, last=False):
                for m in range(FT + 1):
                    if m < FT:
                        dve.wait_ge(filled, 4 * FT * b + (2 * m + 2))
                        dve.wait_ge(gate_done, FT * b + (m + 1))
                        nc.vector.scalar_tensor_tensor(out=whole[:, m % NWH, :], in0=bank[:, (2 * m + 1) % NBK, :],
                                                       scalar=sc[:, 1, m:m + 1], in1=gate[:, m % 2, :], op0=ALU.mult,
                                                       op1=ALU.mult).then_inc(gated, 1)
                    if m > 0:
                        lo(b, m - 1, act_a)
                for n in range(FT, 3 * FT):
                    lo(b, n, act_b if n < 2 * FT else act_a)
                    if n == FT + 1 and not first:
                        finish(b - 1, 1 - u)
                if not last:
                    x_parts(b + 1)

            nc.vector.tensor_scalar(low_bits[:], low_bits[:], LO_MASK, None, ALU.bitwise_and).then_inc(flag_steps, 1)
            dve.wait_ge(flag_steps, 1)
            nc.vector.tensor_reduce(low[:], low_bits[:], AX.X, ALU.max).then_inc(flag_steps, 1)
            dve.wait_ge(flag_across, 1)
            nc.vector.tensor_reduce(low[0:1, :], bank_x[0:1, 0, 0:P], AX.X, ALU.max).then_inc(flag_steps, 1)
            dve.wait_ge(flag_steps, 3)
            nc.vector.tensor_scalar(general[:], low[0:1, :], 1.0, None, ALU.min).then_inc(flag_steps, 1)

            dve.wait_ge(sc_loaded, 80)
            x_parts(0)
            for i in (0, 1, 3):
                dve.wait_ge(w_loaded[i], 16)
                at, cols = WF_AT[i]
                nc.vector.tensor_copy(w_r[:, at:at + cols], w_f32[:, at:at + cols]).then_inc(w_rounded[i], 1)
            seqs(dve, seq)
            finish(NB - 1, 1)


def kernel(**inputs):
    import concourse.bacc as bacc
    from concourse.bass_utils import run_bass_kernel_spmd

    f32 = np.float32
    got = {k: np.asarray(v) for k, v in inputs.items()}
    A, B = "L0_attn_", "L0_ffn_"

    def even_odd(w):
        return w.reshape(NG, GH, DH // 2, 2, L).transpose(4, 0, 3, 1, 2).reshape(L, H * DH)

    inv_freq = 1.0 / 10000.0 ** (np.arange(0, DH, 2, dtype=f32) / DH)
    freqs = np.outer(np.arange(S, dtype=f32), inv_freq)
    twice = np.concatenate([freqs, freqs], -1)[:, ::2]
    rope = np.stack([np.tile(fn(twice).T, (GH, 1)) for fn in (np.cos, np.sin)], 1).astype(f32)

    def per_partition(v):
        return v.reshape(-1, P).T

    def k_tiles(w):
        return w.reshape(w.shape[0], -1, P).transpose(2, 1, 0).reshape(P, -1)

    arrays = {
        "x": got[A + "x"],
        "w_dn": np.concatenate([got[A + "w_down_q"].T, got[A + "w_down_kv"].T], 1),
        "w_upq": even_odd(got[A + "w_up_q"]), "w_upk": even_odd(got[A + "w_up_k"]),
        "w_upv": got[A + "w_up_v"].T, "w_o": got[A + "w_out"].T,
        "ln_sb": np.stack([per_partition(got[A + "ln_scale"]), per_partition(got[A + "ln_bias"])], 1),
        "rope": rope,
        "wf": np.concatenate([k_tiles(got[B + n + "_w"]) for n in ("w1", "w2", "h1", "h2", "w3")], 1),
        "s1": per_partition(got[B + "w1_s"]), "s2": per_partition(got[B + "w2_s"]),
        "sh1": per_partition(got[B + "h1_s"]), "sh2": per_partition(got[B + "h2_s"]),
        "s3": per_partition(got[B + "w3_s"]),
    }
    arrays = {k: np.ascontiguousarray(v) for k, v in arrays.items()}
    nc = bacc.Bacc("TRN2", target_bir_lowering=False, num_devices=1)
    args = [nc.dram_tensor(k, v.shape, mybir.dt.from_np(v.dtype), kind="ExternalInput").ap() for k, v in arrays.items()]
    out = nc.dram_tensor("out", (NB, S, D), F32, kind="ExternalOutput").ap()
    build(nc, *args, out)
    return run_bass_kernel_spmd(nc, [arrays], core_ids=[0]).results[0]["out"]
```

```python
from contextlib import ExitStack

import numpy as np

import concourse.bass as bass
from concourse import mybir

F32 = mybir.dt.float32
F32R = mybir.dt.float32r
I32 = mybir.dt.int32
ACT = mybir.ActivationFunctionType
ALU = mybir.AluOpType
AX = mybir.AxisListType

P = 128
NB, S, D = 8, 512, 256
H, DH = 16, 64
L = 128
F = 1024
TT = S // P
DT = D // P
FT = F // P
NG, GH = 4, 4
HP = H // 2
EPS = 1e-5
RSQRT_MAGIC = 1597463007.0
NEWTON = 3
LN_STEPS = 2 * TT + 2 + 4 * NEWTON + TT

PROLOGUE = ([("hT", 0), ("hT", 1), ("c", 0), ("c", 1)] + [("qk", w, e, 0) for w in range(2) for e in range(2)]
            + [("v", t, 0) for t in range(TT)])
PROLOGUE_LATE = [("qk", 0, e, 1) for e in range(2)]
PER_SEQ = {"hT": DT, "c": 2, "v": 2 * TT, "qk": 4 * NG, "rb": HP, "ot": DT, "ob": TT // 2}


def nth(b, key):
    what = key[0]
    at = {"v": lambda t, half: TT * half + t, "qk": lambda w, e, g: 4 * g + 2 * w + e}.get(what, lambda i: i)(*key[1:])
    return PER_SEQ[what] * b + (at + 1)


def qk(w, g):
    return [("qk", w, 0, g), ("qk", w, 1, g)]


SCHED = [
    ([('qk', 1, 0, 1), ('qk', 1, 1, 1)], [('rb', 7)], [('oh', 0, 0)], []),
    ([('oh', 0, 1), ('oh', 0, 2), ('ot', 0)], [], [('oh', 1, 0), ('oh', 1, 1), ('oh', 1, 2)], []),
    ([('ot', 1)], [], [('qk', 0, 0, 2), ('qk', 0, 1, 2), ('rb', 0), ('ob', 0)], []),
    ([('ob', 1)], [], [], []),
    ([('qk', 1, 0, 2), ('qk', 1, 1, 2)], [('rb', 1)], [], []),
    ([('v', 0, 1)], [('v', 1, 1)], [('v', 2, 1)], []),
    ([('qk', 0, 0, 3), ('qk', 0, 1, 3)], [], [('v', 3, 1)], [('rb', 2), ('hT', 0)]),
    ([], [], [('hT', 1)], []),
    ([('qk', 1, 0, 3), ('qk', 1, 1, 3)], [('rb', 3)], [], []),
    ([], [('c', 0)], [('c', 1)], []),
    ([('qk', 0, 0, 0), ('qk', 0, 1, 0)], [('rb', 4)], [], [('v', 0, 0)]),
    ([], [], [('v', 1, 0)], []),
    ([('qk', 1, 0, 0), ('qk', 1, 1, 0)], [], [('rb', 5)], []),
    ([('v', 2, 0)], [('v', 3, 0)], [], []),
    ([('rb', 6), ('qk', 0, 0, 1), ('qk', 0, 1, 1)], [], [], []),
    ([], [], [], []),
]
NPLACE = 4
OT = 4
LN_PIECE = 4
LN1_STEP, LN2_STEP = 1, 4
LN2_STORE, XR_LOAD = 7, 8
OF_PREV = [("rb", 7)] + [("oh", d, i) if i < 3 else ("ot", d) for d in range(2) for i in range(4)] + [("ob", 0), ("ob", 1)]
OF_NEXT = PROLOGUE + PROLOGUE_LATE
LAST_USE = [key for places in SCHED for place in places for key in place][-1]

SLOTS = 2 * GH
QK_READS = 4


WF_AT, WF_COLS = [], 0
for _cols in (DT * F, DT * F, FT * F, FT * F, FT * D):
    WF_AT.append((WF_COLS, _cols))
    WF_COLS += _cols
LO_MASK = 0xFFF
CHUNK = 256
CHECKS = [(8, 10, 4 * CHUNK), (11, 13, 4 * CHUNK), (14, 15, 3 * CHUNK)]
PER_SEQ_CHUNKS = sum(width for _, _, width in CHECKS) // CHUNK
assert NB * sum(width for _, _, width in CHECKS) == WF_COLS
NBK, NWH = 4, 4
BACK = TT // 2


def build(nc, x, w_dn, w_upq, w_upk, w_upv, w_o, ln_sb, rope, wf, s1, s2, sh1, sh2, s3, out):
    x1_dram = nc.dram_tensor("x1_dram", (NB, P, TT * D), F32, kind="Internal").ap()
    ident_sem = nc.alloc_semaphore("ident_built")
    with ExitStack() as keep:
        ident = keep.enter_context(nc.sbuf_tensor("ident", [P, P], F32))
        low_bits = keep.enter_context(nc.sbuf_tensor("low_bits", [P, CHUNK], I32))
        with nc.sbuf_tensor("w_f32", [P, WF_COLS], F32) as w_f32:
            pass
        wf_loaded = [nc.alloc_semaphore(f"wf{i}_loaded") for i in range(len(WF_AT))]
        attention(nc, x, w_dn, w_upq, w_upk, w_upv, w_o, ln_sb, rope, x1_dram, ident, ident_sem, wf, low_bits,
                  w_f32, wf_loaded)
        ffn(nc, x1_dram, wf, w_f32, wf_loaded, s1, s2, sh1, sh2, s3, out, ident, low_bits)


def layernorm(nc, dve, rows, dst, stats, mv, ve, y, t, chain, base):
    n = [0]
    wait_for = [0]

    def link(op, *args, last=False):
        if wait_for[0]:
            dve.wait_ge(chain, base + wait_for[0])
            wait_for[0] = 0
        op(*args).then_inc(chain, 1)
        n[0] += 1
        if last:
            wait_for[0] = n[0]

    v = nc.vector
    for i in range(TT):
        yield link(v.bn_stats, stats[:, i, :], rows[:, i, :], last=i == TT - 1)
    dve.wait_ge(chain, base + TT)
    wait_for[0] = 0
    nc.vector.memset(t[:], 0.0)
    for i in range(TT):
        yield link(v.bn_aggr, mv[:, i, :], stats[:, i, :], last=i == TT - 1)
    yield link(v.tensor_scalar, ve[:], mv[:, :, 1], EPS, None, ALU.add, last=True)
    yield link(v.tensor_scalar, y[:].bitcast(I32), ve[:].bitcast(I32), -0.5, RSQRT_MAGIC, ALU.mult, ALU.add, last=True)
    for _ in range(NEWTON):
        yield link(v.tensor_tensor, t[:], y[:], y[:], ALU.mult, last=True)
        yield link(v.tensor_tensor, t[:], t[:], ve[:], ALU.mult, last=True)
        yield link(v.tensor_scalar, t[:], t[:], -0.5, 1.5, ALU.mult, ALU.add, last=True)
        yield link(v.tensor_tensor, y[:], y[:], t[:], ALU.mult, last=True)
    for i in range(TT):
        yield link(v.tensor_scalar, dst[:, i, :], rows[:, i, :], mv[:, i, 0:1], y[:, i:i + 1], ALU.subtract, ALU.mult)
    assert n[0] == LN_STEPS


def all_of(steps):
    for _ in steps:
        pass


def attention(nc, x, w_dn, w_upq, w_upk, w_upv, w_o, ln_sb, rope, x1_dram, ident, ident_built, wf, low_bits,
              w_f32, wf_loaded):
    with ExitStack() as ctx:
        def sb(name, shape, dt=F32):
            return ctx.enter_context(nc.sbuf_tensor(name, shape, dt))

        def psum(name, shape):
            return ctx.enter_context(nc.psum_tensor(name, shape, F32))

        def sem(name):
            return ctx.enter_context(nc.semaphore(name))

        q_st = sb("q_st", [P, SLOTS, S], F32R)
        k_st = sb("k_st", [P, SLOTS, 2, S], F32R)
        v_st = sb("v_st", [P, TT, H, 2 * DH], F32R)
        ex = sb("ex", [P, 2, TT, S])
        wdn = sb("wdn", [P, DT, 2 * L])
        wqk_hi = sb("wqk_hi", [P, 2, H * DH], F32R)
        wqk_lo = sb("wqk_lo", [P, 2, H * DH], F32R)
        wv_hi = sb("wv_hi", [P, H * DH], F32R)
        wv_lo = sb("wv_lo", [P, H * DH], F32R)
        wo = sb("wo", [P, HP, D])
        lnsb = sb("lnsb", [P, 2, DT])
        cs = sb("cs", [P, 2, S])
        xn = sb("xn", [P, TT, D])
        xr = sb("xr", [P, TT, D])
        c_hi = sb("c_hi", [P, 2, S], F32R)
        c_lo = sb("c_lo", [P, 2, S], F32R)
        rq = sb("rq", [P, 2, S])
        rm = sb("rm", [P, 4, S])
        hl = sb("hl", [P, 2, 2, S], F32R)
        pt_hi = sb("pt_hi", [P, 2, S], F32R)
        pt_lo = sb("pt_lo", [P, 2, S], F32R)
        ua = sb("ua", [P, S])
        ub = sb("ub", [P, S])
        at = sb("at", [P, HP, S])
        negmax = sb("negmax", [P, 2, TT])
        rsum = sb("rsum", [P, H, TT])
        rinv = sb("rinv", [P, H, TT])
        rinv_b = sb("rinv_b", [P, TT, 2, DH])
        ln_t = [sb(f"ln_{n}", s) for n, s in (("st", [P, TT, 6]), ("mv", [P, TT, 2]), ("ve", [P, TT]),
                                              ("y", [P, TT]), ("t", [P, TT]))]
        hT = sb("hT", [P, DT, S])
        raw = at

        ps_s = psum("ps_s", [P, TT, S])
        ps_t = psum("ps_t", [P, 2, S])
        ps_v = psum("ps_v", [P, S])
        ps_m = psum("ps_m", [P, S])

        w_loaded = sem("w_loaded")
        up_loaded = [sem(f"up{i}_loaded") for i in range(3)]
        w_hi_done = sem("w_hi_done")
        w_lo_done = sem("w_lo_done")
        xn_loaded = sem("xn_loaded")
        xr_loaded = sem("xr_loaded")
        ln1_chain = sem("ln1_chain")
        ln2_chain = sem("ln2_chain")
        x1_stored = sem("x1_stored")
        ready = {what: sem(f"{what}_ready") for what in PER_SEQ}
        done = {what: sem(f"{what}_done") for what in PER_SEQ}
        c_hi_done = sem("c_hi_done")
        v_hi_done = sem("v_hi_done")
        rope_mul = sem("rope_mul")
        rope_add = sem("rope_add")
        rope_hi = sem("rope_hi")
        rope_lo = sem("rope_lo")
        parked = sem("parked")
        placed = [[sem(f"placed_{n}{s}") for s in range(2)] for n in "qk"]
        s_ready = sem("s_ready")
        max_done = sem("max_done")
        exp_done = sem("exp_done")
        t_ready = sem("t_ready")
        pt_hi_done = sem("pt_hi_done")
        pt_lo_done = sem("pt_lo_done")
        pv_done = sem("pv_done")
        pv_copied = sem("pv_copied")
        u_summed = sem("u_summed")
        rinv_done = sem("rinv_done")
        rinv_b_done = sem("rinv_b_done")

        chunk_loaded = sem("chunk_loaded")
        chunk_seen = sem("chunk_seen")

        park = [[nc.dram_tensor(f"park_{n}{i}", (P, 4 * S), F32, kind="Internal").ap() for i in range(2)] for n in "qk"]
        x_v = x.rearrange("b (t p) d -> b p t d", p=P)
        wf_v = wf.rearrange("p (b n) -> b p n", b=NB)
        x1_v = x1_dram.rearrange("b p (t d) -> b p t d", t=TT)

        def seqs(eng, body, prologue, epilogue):
            prologue()
            body(0, first=True)
            with eng.Fori(1, NB - 1) as b:
                body(b)
            body(NB - 1, last=True)
            epilogue()

        def keys(h, place, first, last):
            for key in SCHED[h][place]:
                of = -1 if key in OF_PREV else 1 if key in OF_NEXT else 0
                if not (first and of < 0) and not (last and of > 0):
                    yield key, of

        def rotate(eng, ops, b, w, g):
            eng.wait_ge(done["qk"], nth(b, ("qk", w, 1, g)))
            if not isinstance(b, int) or b + w + g > 0:
                eng.wait_ge(rope_lo, 2 * NG * b + (2 * g + w))
            cos, sin = cs[:, 0, :], cs[:, 1, :]
            ops.tensor_tensor(rm[:, 0, :], rq[:, 0, :], cos, ALU.mult)
            ops.tensor_tensor(rm[:, 1, :], rq[:, 0, :], sin, ALU.mult).then_inc(rope_mul, 1)
            ops.tensor_tensor(rm[:, 2, :], rq[:, 1, :], sin, ALU.mult)
            ops.tensor_tensor(rm[:, 3, :], rq[:, 1, :], cos, ALU.mult).then_inc(rope_mul, 1)
            eng.wait_ge(rope_mul, 4 * NG * b + 2 * (2 * g + w + 1))
            ops.tensor_tensor(rm[:, 0, :], rm[:, 0, :], rm[:, 2, :], ALU.subtract)
            ops.tensor_tensor(rm[:, 1, :], rm[:, 1, :], rm[:, 3, :], ALU.add).then_inc(rope_add, 1)

        def rope_los(eng, ops, b, w, g):
            eng.wait_ge(rope_hi, 2 * NG * b + (2 * g + w + 1))
            ops.tensor_tensor(hl[:, :, 1, :], rm[:, 0:2, :], hl[:, :, 0, :].bitcast(F32),
                                    ALU.subtract).then_inc(rope_lo, 1)

        block = ctx.enter_context(nc.Block())

        @block.sync
        def _(sp):
            def moves(b, w, g):
                sp.wait_ge(rope_lo, 2 * NG * b + (2 * g + w + 1))
                spot = park[w][g % 2]
                sp.dma_start(spot, hl[:].rearrange("p e a s -> p (e a s)").bitcast(F32)).then_inc(parked, 16)
                sp.wait_ge(parked, 32 * NG * b + 16 * (2 * g + w + 1))
                s0 = GH * (g % 2)
                blocks = spot.rearrange("(j r) (e a s) -> a e r j s", j=GH, a=2, e=2)
                both = spot.rearrange("(j r) (e z) -> e r j z", j=GH, e=2)
                for half in range(2):
                    for e in range(2):
                        r0 = 64 * half + 32 * e
                        if w == 0:
                            sp.dma_start(q_st[r0:r0 + 32, s0:s0 + GH, :].bitcast(F32),
                                         blocks[half, e]).then_inc(placed[w][g % 2], 16)
                        else:
                            sp.dma_start(k_st[r0:r0 + 32, s0:s0 + GH].rearrange("r j a s -> r j (a s)").bitcast(F32),
                                         both[e]).then_inc(placed[w][g % 2], 16)

            def load_xn(b):
                sp.dma_start(xn[:], x_v[b]).then_inc(xn_loaded, 16)

            def load_xr(b):
                sp.dma_start(xr[:], x_v[b]).then_inc(xr_loaded, 16)

            def prologue():
                sp.dma_start(xn[:], x_v[0]).then_inc(xn_loaded, 16)
                sp.dma_start(lnsb[:], ln_sb).then_inc(w_loaded, 16)
                sp.dma_start(wdn[:], w_dn.rearrange("(k p) n -> p k n", p=P)).then_inc(w_loaded, 16)
                for i, w in enumerate((w_upq, w_upk, w_upv)):
                    sp.dma_start(raw[:, 2 * i:2 * i + 2, :], w.rearrange("p (a s) -> p a s", s=S)).then_inc(up_loaded[i], 16)
                sp.dma_start(cs[:], rope).then_inc(w_loaded, 16)
                sp.dma_start(wo[:], w_o.rearrange("(k p) n -> p k n", p=P)).then_inc(w_loaded, 16)
                load_xr(0)
                sp.wait_ge(done["hT"], DT)
                load_xn(1)
                for w, g in ((0, 0), (1, 0), (0, 1)):
                    moves(0, w, g)

            def load_wf(parts):
                for i in parts:
                    at, cols = WF_AT[i]
                    sp.dma_start(w_f32[:, at:at + cols], wf[:, at:at + cols]).then_inc(wf_loaded[i], 16)

            def store_x1(b):
                sp.wait_ge(ln2_chain, LN_STEPS * (b + 1))
                sp.dma_start(x1_v[b], xr[:]).then_inc(x1_stored, 16)

            def body(b, first=False, last=False):
                for h in range(H):
                    for i, (at, _, width) in enumerate(CHECKS):
                        if h == at:
                            if i == 0 and not last:
                                sp.wait_ge(done["hT"], DT * b + 2 * DT)
                            else:
                                sp.wait_ge(chunk_seen, PER_SEQ_CHUNKS * b + (4 * i + 1))
                            sp.dma_start(xn[:].rearrange("p t d -> p (t d)")[:, 0:width],
                                         wf_v[b][:, 4 * CHUNK * i:4 * CHUNK * i + width]).then_inc(chunk_loaded, 16)
                    if h == 0 and not last and not first:
                        sp.wait_ge(chunk_seen, PER_SEQ_CHUNKS * b + 1)
                        load_xn(b + 1)
                    if h == LN2_STORE and not first:
                        store_x1(b - 1)
                    if h == XR_LOAD and not first:
                        sp.wait_ge(x1_stored, 16 * b)
                        load_xr(b)
                    for place in range(NPLACE):
                        for key, of in keys(h, place, first, last):
                            if key[0] == "qk" and key[2] == 1:
                                moves(b + of, key[1], key[3])

            def epilogue():
                sp.wait_ge(s_ready, 2 * H * NB)
                load_wf((0, 1, 2))
                sp.wait_ge(pv_done, TT * H * NB)
                load_wf((3, 4))
                store_x1(NB - 1)
                sp.wait_ge(x1_stored, 16 * NB)

            seqs(sp, body, prologue, epilogue)

        @block.tensor
        def _(pe):
            before = [None]

            def misc(b, key):
                what = key[0]
                if what in ("oh", "ot"):
                    d = key[1]
                    i = OT - 1 if what == "ot" else key[2]
                    if what == "oh" and i == 0:
                        pe.wait_ge(done[before[0][1][0]], nth(*before[0]))
                        pe.wait_ge(done["rb"], HP * b + HP)
                    for p in range(HP // OT * i, HP // OT * (i + 1)):
                        ins = nc.tensor.matmul(ps_m[:], wo[:, p, d * P:(d + 1) * P], at[:, p, :],
                                               start=p == 0, stop=p == HP - 1)
                    if what == "ot":
                        before[0] = (b, key)
                        ins.then_inc(ready[what], 1)
                    return
                if before[0]:
                    pe.wait_ge(done[before[0][1][0]], nth(*before[0]))
                before[0] = (b, key)
                what = key[0]
                if what == "hT":
                    pe.wait_ge(ln1_chain, LN_STEPS * (b + 1))
                    for t in range(TT):
                        ins = nc.tensor.transpose(ps_m[:, t * P:(t + 1) * P], xn[:, t, key[1] * P:(key[1] + 1) * P], ident[:])
                elif what == "c":
                    pe.wait_ge(done["hT"], DT * b + DT)
                    for k in range(DT):
                        ins = nc.tensor.matmul(ps_m[:], wdn[:, k, key[1] * L:(key[1] + 1) * L], hT[:, k, :],
                                               start=k == 0, stop=k == DT - 1)
                elif what == "v":
                    pe.wait_ge(done["c"], 2 * b + 2)
                    t, half = key[1], key[2]
                    lhs = (c_hi, c_hi, c_lo)
                    rhs = (wv_hi, wv_lo, wv_hi)
                    for i in range(3):
                        ins = nc.tensor.matmul(ps_m[:], lhs[i][:, 1, t * P:(t + 1) * P],
                                               rhs[i][:, half * S:(half + 1) * S], start=i == 0, stop=i == 2)
                elif what == "qk":
                    pe.wait_ge(done["c"], 2 * b + 2)
                    w, e, g = key[1:]
                    col = (2 * g + e) * P
                    lhs = (wqk_hi, wqk_lo, wqk_hi)
                    rhs = (c_hi, c_hi, c_lo)
                    for i in range(3):
                        ins = nc.tensor.matmul(ps_m[:], lhs[i][:, w, col:col + P], rhs[i][:, w, :],
                                               start=i == 0, stop=i == 2)
                elif what == "rb":
                    p = key[1]
                    pe.wait_ge(rinv_b_done, HP * b + p + 1)
                    for t in range(TT):
                        ins = nc.tensor.transpose(ps_m[:, t * P:(t + 1) * P],
                                                  rinv_b[:, t].rearrange("p h d -> p (h d)"), ident[:])
                elif what == "ob":
                    pe.wait_ge(done["ot"], DT * b + DT)
                    for i in range(2):
                        t = 2 * key[1] + i
                        for d in range(DT):
                            ins = nc.tensor.transpose(ps_m[:, i * D + d * P:i * D + (d + 1) * P],
                                                      hT[:, d, t * P:(t + 1) * P], ident[:])
                ins.then_inc(ready[what], 1)

            def scores(b, h, pair):
                slot, g = h % SLOTS, h // GH
                if pair == 0 and h % GH == 0:
                    for w in range(2):
                        pe.wait_ge(placed[w][g % 2], 16 * QK_READS * (NG // 2 * b + (g // 2 + 1)))
                if h > 0:
                    pe.wait_ge(exp_done, TT * H * b + TT * (h - 1) + 2 * pair + 2)
                elif not (isinstance(b, int) and b == 0):
                    pe.wait_ge(exp_done, TT * H * b + (2 * pair - 2))
                for i in range(2):
                    t = 2 * pair + i
                    for part in range(2):
                        ins = nc.tensor.matmul(ps_s[:, t, :], q_st[:, slot, t * P:(t + 1) * P], k_st[:, slot, part, :],
                                               start=part == 0, stop=part == 1)
                ins.then_inc(s_ready, 1)

            def transposes(b, h, kt):
                n = TT * h + kt
                if kt == 0:
                    pe.wait_ge(exp_done, TT * H * b + TT * (h + 1))
                if n >= 2:
                    pe.wait_ge(pt_lo_done, TT * H * b + n - 1)
                for t in range(TT):
                    ins = nc.tensor.transpose(ps_t[:, kt % 2, t * P:(t + 1) * P], ex[:, h % 2, t, kt * P:(kt + 1) * P], ident[:])
                ins.then_inc(t_ready, 1)

            def values(b, h, kt):
                if kt == 0:
                    pe.wait_ge(pv_copied, H * b + h)
                    if h == 0:
                        pe.wait_ge(done["v"], 2 * TT * b + TT)
                    if h == H // 2:
                        pe.wait_ge(done["v"], 2 * TT * b + 2 * TT)
                pe.wait_ge(pt_lo_done, TT * H * b + TT * h + kt + 1)
                nc.tensor.matmul(ps_v[:], v_st[:, kt, h, :], pt_hi[:, kt % 2, :], start=kt == 0, stop=False)
                nc.tensor.matmul(ps_v[:], v_st[:, kt, h, :], pt_lo[:, kt % 2, :], start=False,
                                 stop=kt == TT - 1).then_inc(pv_done, 1)

            def prologue():
                pe.wait_ge(ident_built, 2)
                for key in PROLOGUE:
                    if key == ("c", 0):
                        pe.wait_ge(w_loaded, 64)
                    if key == PROLOGUE[DT + 2]:
                        pe.wait_ge(w_lo_done, 3)
                    misc(0, key)
                scores(0, 0, 0)
                scores(0, 0, 1)
                for key in PROLOGUE_LATE:
                    misc(0, key)

            def body(b, first=False, last=False):
                if not first:
                    before[0] = (b, LAST_USE)

                def place(h, i):
                    for key, of in keys(h, i, first, last):
                        misc(b + of, key)

                def next_scores(h, pair):
                    if h + 1 < H:
                        scores(b, h + 1, pair)
                    elif not last:
                        scores(b + 1, 0, pair)

                for h in range(H):
                    next_scores(h, 0)
                    transposes(b, h, 0)
                    transposes(b, h, 1)
                    place(h, 0)
                    next_scores(h, 1)
                    transposes(b, h, 2)
                    values(b, h, 0)
                    place(h, 1)
                    values(b, h, 1)
                    transposes(b, h, 3)
                    place(h, 2)
                    values(b, h, 2)
                    values(b, h, 3)
                    place(h, 3)

            def epilogue():
                for key in OF_PREV:
                    misc(NB - 1, key)

            seqs(pe, body, prologue, epilogue)

        @block.scalar
        def _(act):
            def exps(b, h, pair):
                act.wait_ge(max_done, 2 * H * b + (2 * h + pair + 1))
                for t in (2 * pair, 2 * pair + 1):
                    nc.scalar.activation(ex[:, h % 2, t, :], ps_s[:, t, :], ACT.Exp, bias=negmax[:, h % 2, t:t + 1],
                                         accum_out=rsum[:, h, t:t + 1]).then_inc(exp_done, 1)

            def pt_his(b, h, kt):
                n = TT * h + kt
                act.wait_ge(t_ready, TT * H * b + (n + 1))
                if n >= 2:
                    act.wait_ge(pv_done, TT * H * b + (n - 1))
                nc.scalar.activation(pt_hi[:, kt % 2, :], ps_t[:, kt % 2, :], ACT.Copy).then_inc(pt_hi_done, 1)

            def copy_pv(b, h):
                act.wait_ge(pv_done, TT * H * b + (TT * h + TT))
                act.wait_ge(done["rb"], HP * b + h // 2)
                r = DH * (h % 2)
                nc.scalar.activation(ua[r:r + DH, :], ps_v[0:DH, :], ACT.Copy)
                nc.scalar.activation(ub[r:r + DH, :], ps_v[DH:2 * DH, :], ACT.Copy).then_inc(pv_copied, 1)

            def rope_his(b, w, g):
                act.wait_ge(rope_add, 2 * NG * b + (2 * g + w + 1))
                act.wait_ge(parked, 32 * NG * b + 16 * (2 * g + w))
                nc.scalar.activation(hl[:, :, 0, :], rm[:, 0:2, :], ACT.Copy).then_inc(rope_hi, 1)

            def misc(b, key):
                what = key[0]
                if what in ("c", "v", "ot", "qk"):
                    act.wait_ge(ready[what], nth(b, key))
                if what == "c":
                    nc.scalar.activation(c_hi[:, key[1], :], ps_m[:], ACT.Copy).then_inc(c_hi_done, 1)
                elif what == "v":
                    t, half = key[1:]
                    nc.scalar.activation(v_st[:, t, half * (H // 2):(half + 1) * (H // 2), 0:DH],
                                         ps_m[:].rearrange("p (h d) -> p h d", d=DH), ACT.Copy).then_inc(v_hi_done, 1)
                elif what == "qk":
                    w, e, g = key[1:]
                    if e == 0:
                        act.wait_ge(rope_mul, 4 * NG * b + 2 * (2 * g + w))
                    nc.scalar.activation(rq[:, e, :], ps_m[:], ACT.Copy).then_inc(done["qk"], 1)
                elif what == "ot":
                    nc.scalar.activation(hT[:, key[1], :], ps_m[:], ACT.Copy).then_inc(done["ot"], 1)

            def prologue():
                for key in PROLOGUE:
                    misc(0, key)
                    if key[0] == "qk" and key[2] == 1:
                        rope_his(0, key[1], key[3])
                exps(0, 0, 0)
                for key in PROLOGUE_LATE:
                    misc(0, key)
                exps(0, 0, 1)
                rope_his(0, 0, 1)

            def body(b, first=False, last=False):
                def place(h, i):
                    for key, of in keys(h, i, first, last):
                        misc(b + of, key)

                def next_exps(h, pair):
                    if h + 1 < H:
                        exps(b, h + 1, pair)
                    elif not last:
                        exps(b + 1, 0, pair)

                def rope(h):
                    if h == 0:
                        return
                    for i in range(NPLACE):
                        for key, of in keys(h - 1, i, first, last):
                            if key[0] == "qk" and key[2] == 1:
                                rope_his(b + of, key[1], key[3])

                def copy_prev(h):
                    if h > 0:
                        copy_pv(b, h - 1)
                    elif not first:
                        copy_pv(b - 1, H - 1)

                for h in range(H):
                    copy_prev(h)
                    pt_his(b, h, 0)
                    pt_his(b, h, 1)
                    place(h, 0)
                    next_exps(h, 0)
                    rope(h)
                    pt_his(b, h, 2)
                    place(h, 1)
                    pt_his(b, h, 3)
                    place(h, 2)
                    next_exps(h, 1)
                    place(h, 3)

            def epilogue():
                copy_pv(NB - 1, H - 1)
                for key in OF_PREV:
                    misc(NB - 1, key)

            seqs(act, body, prologue, epilogue)

        @block.vector
        def _(dve):
            def maxes(b, h, pair):
                dve.wait_ge(s_ready, 2 * H * b + (2 * h + pair + 1))
                nc.vector.tensor_reduce(negmax[:, h % 2, 2 * pair:2 * pair + 2], ps_s[:, 2 * pair:2 * pair + 2, :],
                                        AX.X, ALU.max, negate=True).then_inc(max_done, 1)

            def pt_los(b, h, kt):
                dve.wait_ge(pt_hi_done, TT * H * b + (TT * h + kt + 1))
                nc.vector.tensor_tensor(pt_lo[:, kt % 2, :], ps_t[:, kt % 2, :], pt_hi[:, kt % 2, :].bitcast(F32),
                                        ALU.subtract).then_inc(pt_lo_done, 1)

            def rinvs(b, p):
                dve.wait_ge(exp_done, TT * H * b + TT * 2 * (p + 1))
                r = rinv[:, 2 * p:2 * p + 2, :]
                nc.vector.reciprocal(r, rsum[:, 2 * p:2 * p + 2, :]).then_inc(rinv_done, 1)
                dve.wait_ge(rinv_done, HP * b + (p + 1))
                nc.vector.tensor_copy(rinv_b[:], r.rearrange("p h t -> p t h").unsqueeze(3).broadcast_to([P, TT, 2, DH])
                                      ).then_inc(rinv_b_done, 1)

            def misc(b, key):
                what = key[0]
                if what not in ("ot", "oh", "qk"):
                    dve.wait_ge(ready[what], nth(b, key))
                if what == "hT":
                    d = key[1]
                    nc.vector.tensor_scalar(hT[:, d, :], ps_m[:], lnsb[:, 0, d:d + 1], lnsb[:, 1, d:d + 1],
                                            ALU.mult, ALU.add).then_inc(done["hT"], 1)
                elif what == "c":
                    dve.wait_ge(c_hi_done, 2 * b + (key[1] + 1))
                    nc.vector.tensor_tensor(c_lo[:, key[1], :], ps_m[:], c_hi[:, key[1], :].bitcast(F32),
                                            ALU.subtract).then_inc(done["c"], 1)
                elif what == "v":
                    t, half = key[1:]
                    dve.wait_ge(v_hi_done, nth(b, key))
                    heads = slice_of(half)
                    nc.vector.tensor_tensor(v_st[:, t, heads[0]:heads[1], DH:2 * DH],
                                            ps_m[:].rearrange("p (h d) -> p h d", d=DH),
                                            v_st[:, t, heads[0]:heads[1], 0:DH].bitcast(F32),
                                            ALU.subtract).then_inc(done["v"], 1)
                elif what == "rb":
                    p = key[1]
                    dve.wait_ge(u_summed, HP * b + (p + 1))
                    nc.vector.tensor_tensor(at[:, p, :], ps_m[:], ua[:], ALU.mult).then_inc(done["rb"], 1)
                elif what == "ob":
                    u = key[1]
                    dve.wait_ge(xr_loaded, 16 * b + 16)
                    v = xr[:, 2 * u:2 * u + 2, :].rearrange("p t d -> p (t d)")
                    nc.vector.scalar_tensor_tensor(out=v, in0=v, scalar=2.0, in1=ps_m[:], op0=ALU.mult,
                                                   op1=ALU.add).then_inc(done["ob"], 1)

            def ln1(b):
                dve.wait_ge(xn_loaded, 16 * b + 16)
                return layernorm(nc, dve, xn, xn, *ln_t, ln1_chain, LN_STEPS * b)

            def ln2(b):
                dve.wait_ge(done["ob"], 2 * b + 2)
                return layernorm(nc, dve, xr, xr, *ln_t, ln2_chain, LN_STEPS * b)

            def prologue():
                all_of(ln1(0))
                dve.wait_ge(w_loaded, 64)
                for key in PROLOGUE[:DT]:
                    misc(0, key)
                for i, (hi, lo, scale) in enumerate(((wqk_hi[:, 0], wqk_lo[:, 0], DH ** -0.5),
                                                     (wqk_hi[:, 1], wqk_lo[:, 1], 1.0), (wv_hi[:], wv_lo[:], 1.0))):
                    dve.wait_ge(up_loaded[i], 16)
                    r = raw[:, 2 * i:2 * i + 2, :].rearrange("p a s -> p (a s)")
                    nc.vector.tensor_scalar(hi, r, scale, None, ALU.mult).then_inc(w_hi_done, 1)
                    dve.wait_ge(w_hi_done, i + 1)
                    nc.vector.scalar_tensor_tensor(out=lo, in0=r, scalar=scale, in1=hi.bitcast(F32), op0=ALU.mult,
                                                   op1=ALU.subtract).then_inc(w_lo_done, 1)
                for key in PROLOGUE[DT:]:
                    misc(0, key)
                    if key[0] == "qk" and key[2] == 1:
                        rotate(dve, nc.vector, 0, key[1], key[3])
                        rope_los(dve, nc.vector, 0, key[1], key[3])
                maxes(0, 0, 0)
                maxes(0, 0, 1)
                rotate(dve, nc.vector, 0, 0, 1)
                rope_los(dve, nc.vector, 0, 0, 1)

            def body(b, first=False, last=False):
                def place(h, i):
                    for key, of in keys(h, i, first, last):
                        misc(b + of, key)

                def next_maxes(h, pair):
                    if h + 1 < H:
                        maxes(b, h + 1, pair)
                    elif not last:
                        maxes(b + 1, 0, pair)

                def look(h):
                    for i, (_, at, width) in enumerate(CHECKS):
                        if h == at:
                            dve.wait_ge(chunk_loaded, 16 * len(CHECKS) * b + 16 * (i + 1))
                            for n in range(width // CHUNK):
                                dve.wait_ge(chunk_seen, PER_SEQ_CHUNKS * b + (4 * i + n + 1))
                                nc.vector.tensor_tensor(low_bits[:], low_bits[:], xn[:, n, :].bitcast(I32),
                                                        ALU.bitwise_or).then_inc(chunk_seen, 1)

                norms = [None]

                def piece():
                    if norms[0] is None:
                        return
                    for _ in range(LN_PIECE):
                        if next(norms[0], "end") == "end":
                            norms[0] = None
                            return

                for h in range(H):
                    if h == LN2_STEP and not first:
                        if norms[0]:
                            all_of(norms[0])
                        norms[0] = ln2(b - 1)
                    if h == LN1_STEP and not last:
                        if norms[0]:
                            all_of(norms[0])
                        norms[0] = ln1(b + 1)
                    next_maxes(h, 0)
                    pt_los(b, h, 0)
                    pt_los(b, h, 1)
                    piece()
                    place(h, 0)
                    piece()
                    if h % 2 == 1:
                        rinvs(b, h // 2)
                    next_maxes(h, 1)
                    place(h, 1)
                    pt_los(b, h, 2)
                    pt_los(b, h, 3)
                    place(h, 2)
                    look(h)
                    piece()
                    place(h, 3)
                    piece()

                if norms[0]:
                    all_of(norms[0])

            def epilogue():
                for key in OF_PREV:
                    misc(NB - 1, key)
                all_of(ln2(NB - 1))

            seqs(dve, body, prologue, epilogue)

        @block.gpsimd
        def _(pool):
            def add_parts(b, p):
                pool.wait_ge(pv_copied, H * b + (2 * p + 2))
                nc.gpsimd.tensor_tensor(ua[:], ua[:], ub[:], ALU.add).then_inc(u_summed, 1)

            def prologue():
                nc.gpsimd.memset(ident[:], 0.0).then_inc(ident_built, 1)
                pool.wait_ge(ident_built, 1)
                nc.gpsimd.affine_select(out=ident[:], in_=ident[:], compare_op=ALU.not_equal, fill=1.0, base=0,
                                        pattern=[[-1, P]], channel_multiplier=1).then_inc(ident_built, 1)
                nc.gpsimd.memset(low_bits[:], 0).then_inc(chunk_seen, 1)

            def body(b, first=False, last=False):
                for h in range(H):
                    if h % 2 == 0 and h > 0:
                        add_parts(b, h // 2 - 1)
                    elif h == 0 and not first:
                        add_parts(b - 1, HP - 1)
                    for i in range(NPLACE):
                        for key, of in keys(h, i, first, last):
                            if key[0] == "qk" and key[2] == 1:
                                rotate(pool, nc.gpsimd, b + of, key[1], key[3])
                    for i in range(NPLACE if h else 0):
                        for key, of in keys(h - 1, i, first, last):
                            if key[0] == "qk" and key[2] == 1:
                                rope_los(pool, nc.gpsimd, b + of, key[1], key[3])

            def epilogue():
                add_parts(NB - 1, HP - 1)

            seqs(pool, body, prologue, epilogue)


def slice_of(half):
    return half * (H // 2), (half + 1) * (H // 2)


def ffn(nc, x1_dram, wf, w_f32, w_loaded, s1, s2, sh1, sh2, s3, out, ident, low_bits):
    with ExitStack() as ctx:
        def sb(name, shape, dt=F32):
            return ctx.enter_context(nc.sbuf_tensor(name, shape, dt))

        def sem(name):
            return ctx.enter_context(nc.semaphore(name))

        w_r = sb("w_r", [P, WF_COLS], F32R)
        sc = sb("sc", [P, 4, FT])
        s3_sb = sb("s3_sb", [P, DT])
        xf = [sb(f"xf{i}", [P, TT, D]) for i in range(2)]
        xT = sb("xT", [P, DT, 2, S], F32R)
        act_a = sb("act_a", [P, FT, 2, S], F32R)
        act_b = sb("act_b", [P, FT, 2, S], F32R)
        gate = sb("gate", [P, 2, S])
        whole = sb("whole", [P, NWH, S])
        yT = sb("yT", [P, DT, S])
        low = sb("low", [P, 1])
        general = sb("general", [1, 1], I32)
        ln_t = [sb(f"lnf_{n}", s) for n, s in (("st", [P, TT, 6]), ("mv", [P, TT, 2]), ("ve", [P, TT]),
                                               ("y", [P, TT]), ("t", [P, TT]))]
        bank = ctx.enter_context(nc.psum_tensor("bank", [P, NBK, S], F32))
        bank_y = ctx.enter_context(nc.psum_tensor("bank_y", [P, DT, S], F32))
        bank_x = ctx.enter_context(nc.psum_tensor("bank_x", [P, 2, S], F32))

        w_rounded = [sem(f"wf{i}_rounded") for i in range(len(WF_AT))]
        w_again = sem("w_again")
        sc_loaded = sem("sc_loaded")
        xf_loaded = [sem(f"xf{i}_loaded") for i in range(2)]
        stored = sem("stored")
        flag_steps = sem("flag_steps")
        flag_across = sem("flag_across")
        filled = sem("filled")
        gate_done = sem("gate_done")
        gated = sem("gated")
        gelu_done = sem("gelu_done")
        hi_done = sem("hi_done")
        lo_done = sem("lo_done")
        x_turned = sem("x_turned")
        xT_hi = sem("xT_hi")
        xT_lo = sem("xT_lo")
        y_ready = sem("y_ready")
        y_copied = sem("y_copied")
        y_turned = sem("y_turned")
        y_added = sem("y_added")
        ln_chain = sem("lnf_chain")

        x1_v = x1_dram.rearrange("b p (t d) -> b p t d", t=TT)
        out_v = out.rearrange("b (t p) d -> b p t d", p=P)
        block = ctx.enter_context(nc.Block())

        def seqs(eng, seq):
            seq(0, 0, 1, first=True)
            with eng.Fori(0, NB // 2 - 1) as i:
                seq(2 * i + 1, 1, i + 2)
                seq(2 * i + 2, 0, i + 2)
            seq(NB - 1, 1, None, last=True)

        @block.sync
        def _(sp):
            for i, s in enumerate((s1, s2, sh1, sh2)):
                sp.dma_start(sc[:, i, :], s).then_inc(sc_loaded, 16)
            sp.dma_start(s3_sb[:], s3).then_inc(sc_loaded, 16)
            sp.dma_start(xf[0][:], x1_v[0]).then_inc(xf_loaded[0], 16)
            sp.dma_start(xf[1][:], x1_v[1]).then_inc(xf_loaded[1], 16)

            def store(b, u):
                sp.wait_ge(ln_chain, LN_STEPS * b + LN_STEPS)
                sp.dma_start(out_v[b], xf[u][:]).then_inc(stored, 16)

            def seq(b, u, load, first=False, last=False):
                if not first:
                    store(b - 1, 1 - u)
                    if not last:
                        sp.wait_ge(stored, 16 * b)
                        sp.dma_start(xf[1 - u][:], x1_v[b + 1]).then_inc(xf_loaded[1 - u], 16)

            seqs(sp, seq)
            store(NB - 1, 1)
            sp.wait_ge(stored, 16 * NB)

        @block.tensor
        def _(pe):
            def x_in(u, load):
                pe.wait_ge(xf_loaded[u], 16 * load)
                for d in range(DT):
                    for t in range(TT):
                        ins = nc.tensor.transpose(bank_x[:, d, t * P:(t + 1) * P], xf[u][:, t, d * P:(d + 1) * P],
                                                  ident[:])
                    ins.then_inc(x_turned, 1)

            def back(b):
                for v in range(BACK):
                    for t in (2 * v, 2 * v + 1):
                        for d in range(DT):
                            if t == 0:
                                pe.wait_ge(y_copied, DT * b + d + 1)
                            ins = nc.tensor.transpose(bank_x[:, v, (t % 2) * D + d * P:(t % 2) * D + (d + 1) * P],
                                                      yT[:, d, t * P:(t + 1) * P], ident[:])
                    ins.then_inc(y_turned, 1)

            def network(dt):
                def weights(i, m, k, width):
                    at = WF_AT[i][0] + k * width + m * P
                    return (w_r if dt == F32R else w_f32)[:, at:at + P]

                def product(dst, w, x, k, k_tiles):
                    for part in range(2):
                        xp = x[:, k, part, :] if dt == F32R else x[:, k, part, :].bitcast(F32)
                        ins = nc.tensor.matmul(dst, w, xp, start=k + part == 0, stop=k + part == k_tiles)
                    return ins

                def begin(b, n, first):
                    m = n - NBK
                    if m < 0:
                        if not first:
                            pe.wait_ge(gelu_done, 2 * FT * b + (m + 1))
                    elif m < 2 * FT:
                        pe.wait_ge((gate_done, gated)[m % 2], FT * b + (m // 2 + 1))
                    else:
                        pe.wait_ge(gelu_done, 2 * FT * b + (m - 2 * FT + 1))
                    return bank[:, n % NBK, :]

                def seq(b, u, load, first=False, last=False):
                    for m in range(FT):
                        for j in range(2):
                            if first and m == 0:
                                pe.wait_ge(w_rounded[j], 1)
                            dst = begin(b, 2 * m + j, first)
                            for k in range(DT):
                                if m == 0 and j == 0:
                                    pe.wait_ge(xT_lo, DT * b + (k + 1))
                                ins = product(dst, weights(j, m, k, F), xT, k, DT)
                            ins.then_inc(filled, 1)
                        if m == 1 and not first:
                            back(b - 1)
                    for j, source in enumerate((act_a, act_b)):
                        if first:
                            pe.wait_ge(w_rounded[2 + j], 1)
                        for ms in [(0, 1)] + [(m,) for m in range(2, FT)]:
                            dsts = [begin(b, 2 * FT + FT * j + m, first) for m in ms]
                            for k in range(FT):
                                if ms[0] == 0:
                                    pe.wait_ge(lo_done, 3 * FT * b + (FT * j + k + 1))
                                for m, dst in zip(ms, dsts):
                                    ins = product(dst, weights(2 + j, m, k, F), source, k, FT)
                                    if k == FT - 1:
                                        ins.then_inc(filled, 1)
                    if not last:
                        if not first:
                            pe.wait_ge(y_added, BACK * b)
                        x_in(1 - u, load)
                    if first:
                        pe.wait_ge(w_rounded[4], 1)
                    for k in range(FT):
                        pe.wait_ge(lo_done, 3 * FT * b + (2 * FT + k + 1))
                        for d in range(DT):
                            ins = product(bank_y[:, d, :], weights(4, d, k, D), act_a, k, FT)
                            if k == FT - 1:
                                ins.then_inc(y_ready, 1)

                seqs(pe, seq)

            pe.wait_ge(flag_steps, 2)
            nc.tensor.transpose(bank_x[0:1, 0, 0:P], low[:], ident[:]).then_inc(flag_across, 1)
            pe.wait_ge(flag_steps, 4)
            x_in(0, 1)
            flag = pe.value_load(general[0:1, 0:1], min_val=0, max_val=1)
            with pe.If(flag < 1):
                network(F32R)
            with pe.If(flag > 0):
                pe.wait_ge(w_again, 16)
                network(F32)
            back(NB - 1)

        @block.gpsimd
        def _(pool):
            pool.wait_ge(flag_steps, 4)
            flag = pool.value_load(general[0:1, 0:1], min_val=0, max_val=1)
            with pool.If(flag > 0):
                for i in range(len(WF_AT)):
                    pool.wait_ge(w_rounded[i], 1)
                pool.dma_start(w_f32[:], wf).then_inc(w_again, 16)

        @block.scalar
        def _(act):
            def x_parts(b):
                for d in range(DT):
                    act.wait_ge(x_turned, DT * b + (d + 1))
                    nc.scalar.activation(xT[:, d, 0, :], bank_x[:, d, :], ACT.Copy).then_inc(xT_hi, 1)

            def hi(b, n, dst):
                nc.scalar.activation(dst[:, n % FT, 0, :], whole[:, n % NWH, :], ACT.Copy).then_inc(hi_done, 1)

            def seq(b, u, load, first=False, last=False):
                for m in range(FT + 1):
                    if m < FT:
                        act.wait_ge(filled, 4 * FT * b + (2 * m + 1))
                        if m >= 2:
                            act.wait_ge(gated, FT * b + (m - 1))
                        nc.scalar.activation(gate[:, m % 2, :], bank[:, 2 * m % NBK, :], ACT.Silu,
                                             scale=sc[:, 0, m:m + 1]).then_inc(gate_done, 1)
                    if m > 0:
                        act.wait_ge(gated, FT * b + m)
                        hi(b, m - 1, act_a)
                for j, dst in enumerate((act_b, act_a)):
                    for m in range(FT):
                        n = FT + FT * j + m
                        act.wait_ge(filled, 4 * FT * b + (FT + n + 1))
                        act.wait_ge(lo_done, 3 * FT * b + (n - NWH + 1))
                        nc.scalar.activation(whole[:, n % NWH, :], bank[:, (FT + n) % NBK, :], ACT.Gelu,
                                             scale=sc[:, 2 + j, m:m + 1]).then_inc(gelu_done, 1)
                        act.wait_ge(gelu_done, 2 * FT * b + (n - FT + 1))
                        hi(b, n, dst)
                if not last:
                    x_parts(b + 1)
                for d in range(DT):
                    act.wait_ge(y_ready, DT * b + (d + 1))
                    nc.scalar.activation(yT[:, d, :], bank_y[:, d, :], ACT.Copy,
                                         scale=s3_sb[:, d:d + 1]).then_inc(y_copied, 1)

            act.wait_ge(sc_loaded, 80)
            x_parts(0)
            for i in (2, 4):
                act.wait_ge(w_loaded[i], 16)
                at, cols = WF_AT[i]
                nc.scalar.activation(w_r[:, at:at + cols], w_f32[:, at:at + cols], ACT.Copy).then_inc(w_rounded[i], 1)
            seqs(act, seq)

        @block.vector
        def _(dve):
            def x_parts(b):
                for d in range(DT):
                    dve.wait_ge(xT_hi, DT * b + (d + 1))
                    nc.vector.tensor_tensor(xT[:, d, 1, :], bank_x[:, d, :], xT[:, d, 0, :].bitcast(F32),
                                            ALU.subtract).then_inc(xT_lo, 1)

            def lo(b, n, dst):
                dve.wait_ge(hi_done, 3 * FT * b + (n + 1))
                nc.vector.tensor_tensor(dst[:, n % FT, 1, :], whole[:, n % NWH, :], dst[:, n % FT, 0, :].bitcast(F32),
                                        ALU.subtract).then_inc(lo_done, 1)

            def finish(b, u):
                for v in range(BACK):
                    dve.wait_ge(y_turned, BACK * b + (v + 1))
                    rows = xf[u][:, 2 * v:2 * v + 2, :].rearrange("p t d -> p (t d)")
                    nc.vector.tensor_tensor(rows, rows, bank_x[:, v, :], ALU.add).then_inc(y_added, 1)
                dve.wait_ge(y_added, BACK * b + BACK)
                all_of(layernorm(nc, dve, xf[u], xf[u], *ln_t, ln_chain, LN_STEPS * b))

            def seq(b, u, load, first=False, last=False):
                for m in range(FT + 1):
                    if m < FT:
                        dve.wait_ge(filled, 4 * FT * b + (2 * m + 2))
                        dve.wait_ge(gate_done, FT * b + (m + 1))
                        nc.vector.scalar_tensor_tensor(out=whole[:, m % NWH, :], in0=bank[:, (2 * m + 1) % NBK, :],
                                                       scalar=sc[:, 1, m:m + 1], in1=gate[:, m % 2, :], op0=ALU.mult,
                                                       op1=ALU.mult).then_inc(gated, 1)
                    if m > 0:
                        lo(b, m - 1, act_a)
                for n in range(FT, 3 * FT):
                    lo(b, n, act_b if n < 2 * FT else act_a)
                    if n == FT + 1 and not first:
                        finish(b - 1, 1 - u)
                if not last:
                    x_parts(b + 1)

            nc.vector.tensor_scalar(low_bits[:], low_bits[:], LO_MASK, None, ALU.bitwise_and).then_inc(flag_steps, 1)
            dve.wait_ge(flag_steps, 1)
            nc.vector.tensor_reduce(low[:], low_bits[:], AX.X, ALU.max).then_inc(flag_steps, 1)
            dve.wait_ge(flag_across, 1)
            nc.vector.tensor_reduce(low[0:1, :], bank_x[0:1, 0, 0:P], AX.X, ALU.max).then_inc(flag_steps, 1)
            dve.wait_ge(flag_steps, 3)
            nc.vector.tensor_scalar(general[:], low[0:1, :], 1.0, None, ALU.min).then_inc(flag_steps, 1)

            dve.wait_ge(sc_loaded, 80)
            x_parts(0)
            for i in (0, 1, 3):
                dve.wait_ge(w_loaded[i], 16)
                at, cols = WF_AT[i]
                nc.vector.tensor_copy(w_r[:, at:at + cols], w_f32[:, at:at + cols]).then_inc(w_rounded[i], 1)
            seqs(dve, seq)
            finish(NB - 1, 1)


def kernel(**inputs):
    import concourse.bacc as bacc
    from concourse.bass_utils import run_bass_kernel_spmd

    f32 = np.float32
    got = {k: np.asarray(v) for k, v in inputs.items()}
    A, B = "L0_attn_", "L0_ffn_"

    def even_odd(w):
        return w.reshape(NG, GH, DH // 2, 2, L).transpose(4, 0, 3, 1, 2).reshape(L, H * DH)

    inv_freq = 1.0 / 10000.0 ** (np.arange(0, DH, 2, dtype=f32) / DH)
    freqs = np.outer(np.arange(S, dtype=f32), inv_freq)
    twice = np.concatenate([freqs, freqs], -1)[:, ::2]
    rope = np.stack([np.tile(fn(twice).T, (GH, 1)) for fn in (np.cos, np.sin)], 1).astype(f32)

    def per_partition(v):
        return v.reshape(-1, P).T

    def k_tiles(w):
        return w.reshape(w.shape[0], -1, P).transpose(2, 1, 0).reshape(P, -1)

    arrays = {
        "x": got[A + "x"],
        "w_dn": np.concatenate([got[A + "w_down_q"].T, got[A + "w_down_kv"].T], 1),
        "w_upq": even_odd(got[A + "w_up_q"]), "w_upk": even_odd(got[A + "w_up_k"]),
        "w_upv": got[A + "w_up_v"].T, "w_o": got[A + "w_out"].T,
        "ln_sb": np.stack([per_partition(got[A + "ln_scale"]), per_partition(got[A + "ln_bias"])], 1),
        "rope": rope,
        "wf": np.concatenate([k_tiles(got[B + n + "_w"]) for n in ("w1", "w2", "h1", "h2", "w3")], 1),
        "s1": per_partition(got[B + "w1_s"]), "s2": per_partition(got[B + "w2_s"]),
        "sh1": per_partition(got[B + "h1_s"]), "sh2": per_partition(got[B + "h2_s"]),
        "s3": per_partition(got[B + "w3_s"]),
    }
    arrays = {k: np.ascontiguousarray(v) for k, v in arrays.items()}
    nc = bacc.Bacc("TRN2", target_bir_lowering=False, num_devices=1)
    args = [nc.dram_tensor(k, v.shape, mybir.dt.from_np(v.dtype), kind="ExternalInput").ap() for k, v in arrays.items()]
    out = nc.dram_tensor("out", (NB, S, D), F32, kind="ExternalOutput").ap()
    build(nc, *args, out)
    return run_bass_kernel_spmd(nc, [arrays], core_ids=[0]).results[0]["out"]
```
